# Optimizing a Trainium2 kernel written in Bass

```python
import numpy as np
import jax
import jax.numpy as jnp

def _softmax(x, axis=-1):
    return jax.nn.softmax(x, axis=axis)

def _gelu(x):
    return jax.nn.gelu(x, approximate=True)

def _silu(x):
    return jax.nn.silu(x)

def _sigmoid(x):
    return jax.nn.sigmoid(x)

def _layernorm(x, axis=-1, eps=1e-05):
    m = jnp.mean(x, axis=axis, keepdims=True)
    v = jnp.var(x, axis=axis, keepdims=True)
    return (x - m) / jnp.sqrt(v + eps)

def _scatter_add(tgt, idx, src, axis=0):
    return tgt.at[idx].add(src)

def _segment_sum(src, seg, n):
    return jax.ops.segment_sum(src, seg, n)
kernel_name = 'mk_gnn_preln_d1_gnn_r64_f0c84e'

def setup_inputs(seed: int=0):
    np.random.seed(seed)
    _w = jnp.asarray

    def _rec_inputs():
        import jax
        import jax.numpy as jnp
        _gk = jax.random.key(seed)
        x = -0.0003713 + 1 * jax.random.normal(jax.random.fold_in(_gk, 1), (100000, 256), jnp.float32)
        src = jax.random.randint(jax.random.fold_in(_gk, 2), (25000,), 0, 100000, jnp.int32)
        dst = jnp.minimum((100000 * jax.random.uniform(jax.random.fold_in(_gk, 3), (25000,)) ** 2.0).astype(jnp.int32), 99999)
        _o = jnp.argsort(dst, stable=True)
        src = src[_o]
        dst = dst[_o]
        edge_attr_16 = 0.000254156 + 0.999948 * jax.random.normal(jax.random.fold_in(_gk, 11), (25000, 16), jnp.float32)
        return (x, src, dst, edge_attr_16)
    x, src, dst, edge_attr_16 = _rec_inputs()

    def _L0_gnn_setup():
        import jax, jax.numpy as jnp
        import numpy as np
        N, D, H = (50000, 256, 8)
        HD = D // H
        E = 12500
        NEG_SLOPE = 0.2

        def _gat_layer(x, edge_index, W, att_src, att_dst, bias, ln_g, ln_b, W1, b1, W2, b2):
            n = x.shape[0]
            sl = jnp.arange(n, dtype=edge_index.dtype)
            src = jnp.concatenate([edge_index[0], sl])
            dst = jnp.concatenate([edge_index[1], sl])
            xp = (x @ W).reshape(n, H, HD)
            a_src = jnp.einsum('nhd,hd->nh', xp, att_src)
            a_dst = jnp.einsum('nhd,hd->nh', xp, att_dst)
            e = a_src[src] + a_dst[dst]
            e = jax.nn.leaky_relu(e, NEG_SLOPE)
            m = jax.ops.segment_max(e, dst, num_segments=n)
            ex = jnp.exp(e - m[dst])
            denom = jax.ops.segment_sum(ex, dst, num_segments=n)
            alpha = ex / (denom[dst] + 1e-16)
            msg = alpha[:, :, None] * xp[src]
            out = jax.ops.segment_sum(msg, dst, num_segments=n)
            h = out.reshape(n, D) + bias
            r = h + x
            mu = jnp.mean(r, axis=-1, keepdims=True)
            var = jnp.mean(jnp.square(r - mu), axis=-1, keepdims=True)
            hn = (r - mu) / jnp.sqrt(var + 1e-05) * ln_g + ln_b
            return jax.nn.relu(hn @ W1 + b1) @ W2 + b2
        key = jax.random.key(seed)
        ks = jax.random.split(key, 12)
        s = 1.0 / np.sqrt(D)
        return {'x': jax.random.normal(ks[0], (N, D), jnp.float32), 'edge_index': jax.random.randint(ks[1], (2, E), 0, N, jnp.int64), 'edge_attr': jax.random.normal(ks[2], (E, 16), jnp.float32), 'W': jax.random.normal(ks[3], (D, D), jnp.float32) * s, 'att_src': jax.random.normal(ks[4], (H, HD), jnp.float32) * s, 'att_dst': jax.random.normal(ks[5], (H, HD), jnp.float32) * s, 'bias': jnp.zeros((D,), jnp.float32), 'ln_g': jnp.ones((D,), jnp.float32), 'ln_b': jnp.zeros((D,), jnp.float32), 'W1': jax.random.normal(ks[6], (D, D), jnp.float32) * s, 'b1': jnp.zeros((D,), jnp.float32), 'W2': jax.random.normal(ks[7], (D, D), jnp.float32) * s, 'b2': jnp.zeros((D,), jnp.float32)}
    _L0_gnn_all = _L0_gnn_setup()
    _L0_gnn_in = {k: v for k, v in _L0_gnn_all.items() if k in ('W', 'att_src', 'att_dst', 'bias', 'ln_g', 'ln_b', 'W1', 'b1', 'W2', 'b2')}
    del _L0_gnn_all
    return {'x': x, 'src': src, 'dst': dst, 'edge_attr_16': edge_attr_16, 'L0_gnn_W': _L0_gnn_in['W'], 'L0_gnn_att_src': _L0_gnn_in['att_src'], 'L0_gnn_att_dst': _L0_gnn_in['att_dst'], 'L0_gnn_bias': _L0_gnn_in['bias'], 'L0_gnn_ln_g': _L0_gnn_in['ln_g'], 'L0_gnn_ln_b': _L0_gnn_in['ln_b'], 'L0_gnn_W1': _L0_gnn_in['W1'], 'L0_gnn_b1': _L0_gnn_in['b1'], 'L0_gnn_W2': _L0_gnn_in['W2'], 'L0_gnn_b2': _L0_gnn_in['b2']}

def reference(x, src, dst, edge_attr_16, L0_gnn_W, L0_gnn_att_src, L0_gnn_att_dst, L0_gnn_bias, L0_gnn_ln_g, L0_gnn_ln_b, L0_gnn_W1, L0_gnn_b1, L0_gnn_W2, L0_gnn_b2):
    import jax
    import jax.numpy as jnp

    def _L0_gnn_ref(x, edge_index, edge_attr, W, att_src, att_dst, bias, ln_g, ln_b, W1, b1, W2, b2):
        import jax, jax.numpy as jnp
        import numpy as np
        N, D, H = (50000, 256, 8)
        HD = D // H
        E = 12500
        NEG_SLOPE = 0.2

        def _gat_layer(x, edge_index, W, att_src, att_dst, bias, ln_g, ln_b, W1, b1, W2, b2):
            n = x.shape[0]
            sl = jnp.arange(n, dtype=edge_index.dtype)
            src = jnp.concatenate([edge_index[0], sl])
            dst = jnp.concatenate([edge_index[1], sl])
            xp = (x @ W).reshape(n, H, HD)
            a_src = jnp.einsum('nhd,hd->nh', xp, att_src)
            a_dst = jnp.einsum('nhd,hd->nh', xp, att_dst)
            e = a_src[src] + a_dst[dst]
            e = jax.nn.leaky_relu(e, NEG_SLOPE)
            m = jax.ops.segment_max(e, dst, num_segments=n)
            ex = jnp.exp(e - m[dst])
            denom = jax.ops.segment_sum(ex, dst, num_segments=n)
            alpha = ex / (denom[dst] + 1e-16)
            msg = alpha[:, :, None] * xp[src]
            out = jax.ops.segment_sum(msg, dst, num_segments=n)
            h = out.reshape(n, D) + bias
            r = h + x
            mu = jnp.mean(r, axis=-1, keepdims=True)
            var = jnp.mean(jnp.square(r - mu), axis=-1, keepdims=True)
            hn = (r - mu) / jnp.sqrt(var + 1e-05) * ln_g + ln_b
            return jax.nn.relu(hn @ W1 + b1) @ W2 + b2
        return _gat_layer(x, edge_index, W, att_src, att_dst, bias, ln_g, ln_b, W1, b1, W2, b2)
    edge_index = jnp.stack([src, dst])
    h = jnp.maximum(_layernorm(x, axis=-1), 0.0)
    x = x + _L0_gnn_ref(h, edge_index, edge_attr_16, L0_gnn_W, L0_gnn_att_src, L0_gnn_att_dst, L0_gnn_bias, L0_gnn_ln_g, L0_gnn_ln_b, L0_gnn_W1, L0_gnn_b1, L0_gnn_W2, L0_gnn_b2)
    return x

_drawn_inputs = setup_inputs


def setup_inputs(seed=0):
    import zlib

    import numpy as np

    out = dict(_drawn_inputs(seed))
    spreads = {'L0_gnn_bias': (0.0, 0.1),
     'L0_gnn_ln_g': (1.0, 0.2),
     'L0_gnn_ln_b': (0.0, 0.1),
     'L0_gnn_b1': (0.0, 0.1),
     'L0_gnn_b2': (0.0, 0.1)}
    factors = {'L0_gnn_att_src': 5.22, 'L0_gnn_att_dst': 22.106}
    for name, (base, spread) in spreads.items():
        noise = np.random.default_rng([zlib.crc32(name.encode()), seed]).standard_normal(out[name].shape)
        drawn = base * np.exp(spread * noise) if base else spread * noise
        out[name] = jnp.asarray(drawn.astype(out[name].dtype))
    for name, factor in factors.items():
        out[name] = (out[name] * factor).astype(out[name].dtype)
    return out
```

```python
from contextlib import ExitStack

import concourse.bass as bass
from concourse import mybir

P = 128
F32 = mybir.dt.float32
F32R = mybir.dt.float32r
I32 = mybir.dt.int32
ALU = mybir.AluOpType
ACT = mybir.ActivationFunctionType
AX_X = mybir.AxisListType.X
EPS = 1e-5
SLOPE = 0.2
FAR = 1e30


class Place:

    def __init__(self, number, slot_of, live, looped):
        self.n = number
        self.slot_of = slot_of
        self.live = live
        self.looped = looped

    def slot(self, slots):
        return self.slot_of % slots

    def after(self, k):
        return self.looped or self.n >= k


def pipeline(eng, step, tiles, depth, unroll):
    first = -(-(depth + unroll) // unroll) * unroll
    last = (tiles - 1) // unroll * unroll

    def fixed(s):
        step(lambda lag: Place(s - lag, s - lag + 16 * unroll, 0 <= s - lag < tiles, False))

    for s in range(first):
        fixed(s)
    with eng.Fori(0, (last - first) // unroll) as turn:
        i = turn * unroll + first
        for u in range(unroll):
            step(lambda lag, u=u: Place(i + (u - lag), u - lag + 16 * unroll, True, True))
    for s in range(last, tiles + depth):
        fixed(s)


def gat_kernel(nc, x, src, dst, w, att_src, att_dst, bias, ln_g, ln_b, w1, b1, w2, b2, out):
    N, D = x.shape
    (E,) = src.shape
    H, HD = att_src.shape
    KC = D // P
    C = -(-E // P)
    FULL = E // C
    REST = E - FULL * C
    NR = D + 2 * H
    DH = D + H
    TR = 16
    NB = -(-(N + 2 * P) // (P * TR))
    NT = NB * P * TR
    NONE = N + P
    Q = 4
    CH = P * Q
    NC = -(-N // CH)
    assert KC == 2 and FULL == P - 1 and C % 2 == 0 and NC % 4 == 0 and NT >= NONE + P

    table = nc.dram_tensor("table", [NT, NR], F32, kind="Internal").ap()

    with ExitStack() as whole:
        def sem(name, stack=whole):
            return stack.enter_context(nc.semaphore(name))

        def sb(name, shape, dt=F32, stack=whole):
            return stack.enter_context(nc.sbuf_tensor(name, shape, dt))

        def ps(name, shape, stack):
            return stack.enter_context(nc.psum_tensor(name, shape, F32))

        passed = {nc.vector: sem("passed_vector"), nc.gpsimd: sem("passed_gpsimd")}

        def own_wait(eng):
            eng.sem_inc(passed[eng])

        ident = sb("ident", [P, P])
        below = sb("below", [P, P])
        half = sb("half", [P, 8])
        wd = sb("wd", [P, KC, DH])
        wa = sb("wa", [P, KC, H])
        bias_row = sb("bias_row", [1, DH])
        ones_row = sb("ones_row", [1, P])
        wi = [sb(f"wi{k}", [P, KC, D], F32R) for k in range(2)]
        w1p = [sb(f"w1p{k}", [P, KC, D], F32R) for k in range(2)]
        w2p = [sb(f"w2p{k}", [P, KC, D], F32R) for k in range(2)]
        b1e = sb("b1e", [P, KC])
        b2b = sb("b2b", [P, D])
        x_index = sb("x_index", [P, C, 2], I32)
        d_index = sb("d_index", [P, C], I32)
        d_value = sb("d_value", [P, C, 2])

        with ExitStack() as st:
            wf = sb("wf", [P, KC, D], F32, st)
            w1f = sb("w1f", [P, KC, D], F32, st)
            w2f = sb("w2f", [P, KC, D], F32, st)
            wplus = sb("wplus", [P, KC, D], F32, st)
            w1g = sb("w1g", [P, KC, D], F32, st)
            prod = sb("prod", [P, KC, 2, D], F32, st)
            att = sb("att", [P, 2, D], F32, st)
            wad = sb("wad", [P, KC, 2, H], F32, st)
            gcol = sb("gcol", [P, KC], F32, st)
            lbcol = sb("lbcol", [P, KC], F32, st)
            b1col = sb("b1col", [P, KC], F32, st)
            biasb = sb("biasb", [P, D], F32, st)
            fill = sb("fill", [P, TR, NR], F32, st)
            s_in = sb("s_in", [P, C], I32, st)
            spare = sb("spare", [P, 1], F32, st)
            sparei = sb("sparei", [P, 1], I32, st)
            pb = ps("pb", [P, KC, 512], st)
            padded = sem("padded", st)
            loaded = sem("loaded", st)
            indexed = sem("indexed", st)
            made = sem("made", st)
            folded = sem("folded", st)
            split = sem("split", st)
            turned0 = sem("turned0", st)
            fill_ready = sem("fill_ready", st)
            filled = sem("filled", st)
            block = st.enter_context(nc.Block())
            LOADS = 12

            @block.sync
            def _(sp):
                by_row = "(c p) n -> p c n"
                sp.dma_start(biasb[:], bias.rearrange("(a n) -> a n", a=1).broadcast_to([P, D])).then_inc(loaded, 16)
                sp.dma_start(wf[:], w.rearrange(by_row, p=P)).then_inc(loaded, 16)
                sp.dma_start(w1f[:], w1.rearrange(by_row, p=P)).then_inc(loaded, 16)
                sp.dma_start(w2f[:], w2.rearrange(by_row, p=P)).then_inc(loaded, 16)
                for k, a in enumerate((att_src, att_dst)):
                    sp.dma_start(att[:, k], a.rearrange("(a h) d -> a (h d)", a=1).broadcast_to([P, D])).then_inc(loaded, 16)
                sp.dma_start(b2b[:], b2.rearrange("(a n) -> a n", a=1).broadcast_to([P, D])).then_inc(loaded, 16)
                for col, v in ((gcol, ln_g), (lbcol, ln_b), (b1col, b1)):
                    for c in range(KC):
                        if col is not gcol or c >= 0:
                            sp.dma_start(col[:, c:c + 1], v[c * P:(c + 1) * P].rearrange("(p a) -> p a", a=1)).then_inc(loaded, 16)
                sp.wait_ge(padded, 2)
                for tile, v in ((s_in, src), (d_index, dst)):
                    sp.dma_start(tile[0:FULL, :], v[0:FULL * C].rearrange("(p t) -> p t", t=C)).then_inc(indexed, 16)
                    sp.dma_start(tile[FULL:P, 0:REST], v[FULL * C:E].rearrange("(p t) -> p t", p=1)).then_inc(indexed, 16)
                sp.wait_ge(fill_ready, 1)
                rows = table.rearrange("(b p r) n -> b p (r n)", p=P, r=TR)
                with sp.Fori(0, NB) as b:
                    sp.dma_start(rows[bass.ds(b, 1)].rearrange("a p n -> (a p) n"), fill[:].rearrange("p r n -> p (r n)")).then_inc(filled, 16)
                sp.wait_ge(filled, 16 * NB)

            @block.gpsimd
            def _(pool):
                pool.memset(s_in[:], 0).then_inc(padded, 1)
                pool.memset(d_index[:], NONE).then_inc(padded, 1)
                pool.memset(ident[:], 0.0)
                pool.memset(below[:], 1.0)
                pool.memset(half[:], -0.5)
                pool.memset(ones_row[:], 1.0)
                pool.iota(sparei[:], pattern=[[0, 1]], base=N, channel_multiplier=1).then_inc(made, 1)
                pool.wait_ge(made, 1)
                pool.affine_select(out=ident[:], in_=ident[:], compare_op=ALU.not_equal, fill=1.0, base=0,
                                   pattern=[[-1, P]], channel_multiplier=1)
                pool.affine_select(out=below[:], in_=below[:], compare_op=ALU.is_gt, fill=0.0, base=0,
                                   pattern=[[-1, P]], channel_multiplier=1).then_inc(made, 1)

            @block.vector
            def _(dve):
                dve.wait_ge(loaded, 16 * 13)
                nc.vector.tensor_copy(fill[:, :, 0:D], biasb[:].rearrange("p (a n) -> p a n", a=1).broadcast_to([P, TR, D]))
                nc.vector.memset(fill[:, :, D:NR], 0.0).then_inc(fill_ready, 1)
                nc.vector.tensor_copy(bias_row[:, 0:D], biasb[0:1, :])
                nc.vector.memset(bias_row[:, D:DH], 0.0)
                for c in range(KC):
                    nc.vector.tensor_scalar(w1g[:, c], w1f[:, c], gcol[:, c:c + 1], None, ALU.mult)
                nc.vector.tensor_copy(wd[:, :, 0:D], wf[:])
                for c in range(KC):
                    for k in range(2):
                        ins = nc.vector.tensor_tensor(prod[:, c, k], wf[:, c], att[:, k], ALU.mult)
                ins.then_inc(folded, 1)
                dve.wait_ge(folded, 1)
                nc.vector.tensor_reduce(wad[:], prod[:].rearrange("p c k (h d) -> p c k h d", h=H), AX_X, ALU.add).then_inc(folded, 1)
                dve.wait_ge(made, 2)
                nc.vector.tensor_copy(wplus[:], wf[:])
                nc.vector.tensor_copy(spare[:], sparei[:]).then_inc(folded, 1)
                dve.wait_ge(folded, 3)
                nc.vector.tensor_copy(wd[:, :, D:DH], wad[:, :, 0])
                nc.vector.tensor_tensor(wa[:], wad[:, :, 0], wad[:, :, 1], ALU.add)
                for c in range(KC):
                    diagonal = wplus[:, c, c * P:(c + 1) * P]
                    ins = nc.vector.tensor_tensor(diagonal, diagonal, ident[:], ALU.add)
                ins.then_inc(folded, 1)
                dve.wait_ge(indexed, 64)
                nc.vector.tensor_copy(x_index[:, :, 0], s_in[:])
                nc.vector.tensor_scalar(x_index[:, :, 1], d_index[:], float(N - 1), None, ALU.min)
                nc.vector.tensor_copy(d_value[:, :, 0], d_index[:]).then_inc(folded, 1)
                dve.wait_ge(folded, 5)
                nc.vector.tensor_scalar(d_value[:, :, 1], d_value[:, :, 0], -1.0, spare[:, 0:1], ALU.mult, ALU.add)
                dve.wait_ge(split, 3)
                for parts, whole_w in ((wi, wplus), (w1p, w1g), (w2p, w2f)):
                    nc.vector.tensor_tensor(parts[1][:], whole_w[:], parts[0][:].bitcast(F32), ALU.subtract)
                dve.wait_ge(turned0, 1)
                nc.vector.tensor_tensor(b1e[:], pb[:, :, 0], b1col[:], ALU.add).then_inc(folded, 1)

            @block.scalar
            def _(act):
                act.wait_ge(folded, 4)
                for parts, whole_w in ((wi, wplus), (w1p, w1g), (w2p, w2f)):
                    nc.scalar.activation(parts[0][:], whole_w[:], ACT.Copy).then_inc(split, 1)

            @block.tensor
            def _(pe):
                pe.wait_ge(loaded, 16 * 13)
                for o in range(KC):
                    for c in range(KC):
                        ins = nc.tensor.matmul(pb[:, o, 0:1], w1f[:, c, o * P:(o + 1) * P], lbcol[:, c:c + 1],
                                               start=(c == 0), stop=(c == KC - 1))
                ins.then_inc(turned0, 1)

        with ExitStack() as st:
            gi = sb("gi", [P, 2, 2], I32, st)
            gd = sb("gd", [P, 2, 1], I32, st)
            xg = sb("xg", [P, 2, 2, D], F32, st)
            stats = sb("stats", [P, 2, 2, 6], F32, st)
            mv = sb("mv", [P, 2, 2, 2], F32, st)
            ve = sb("ve", [P, 2, 2], F32, st)
            rstd = sb("rstd", [P, 2, 2], F32, st)
            nmr = sb("nmr", [P, 2, 2], F32, st)
            hg = sb("hg", [P, 2, 2, D], F32, st)
            hdif = sb("hdif", [P, 2, D], F32, st)
            hT = sb("hT", [P, 2, 4, P], F32, st)
            dv = sb("dv", [P, 2, 2], F32, st)
            same = sb("same", [P, 2, P], F32, st)
            apart = sb("apart", [P, P], F32, st)
            lower = sb("lower", [P, P], F32, st)
            dups = sb("dups", [P, 1], F32, st)
            spare_if = sb("spare_if", [P, 1], F32, st)
            si = sb("si", [P, 2, 1], I32, st)
            raw = sb("raw", [P, 3, H], F32, st)
            s_own = sb("s_own", [P, 1, H], F32, st)
            rawsum = sb("rawsum", [P, 3, H], F32, st)
            score = sb("score", [P, 2, 3, H], F32, st)
            shifted = sb("shifted", [P, H], F32, st)
            spread = sb("spread", [P, H, P], F32, st)
            prob = sb("prob", [P, 2, H], F32, st)
            weighed = sb("weighed", [P, 2, DH], F32, st)
            old = sb("old", [P, 2, NR], F32, st)
            new = sb("new", [P, 2, NR], F32, st)
            mine = sb("mine", [P, H], F32, st)
            pair = sb("pair", [P, 2, H], F32, st)
            lold = sb("lold", [P, H], F32, st)
            fade = sb("fade", [P, 2, H], F32, st)
            part = sb("part", [P, 2, H], F32, st)
            recip = sb("recip", [P, H], F32, st)
            scale = sb("scale", [P, 2, H], F32, st)
            kept = sb("kept", [P, D], F32, st)
            added = sb("added", [P, D], F32, st)

            pT = ps("pT", [P, 4, P], st)
            pR = ps("pR", [P, 512], st)
            pS = ps("pS", [P, 512], st)
            pD = ps("pD", [P, 512], st)
            pG = ps("pG", [P, H, P], st)
            pV = [ps(f"pV{k}", [P, 512], st) for k in range(2)]

            idx_ready = sem("idx_ready", st)
            x_landed = [sem(f"x_landed{k}", st) for k in range(2)]
            front = sem("front", st)
            rooted = sem("rooted", st)
            h_made = sem("h_made", st)
            dif_made = sem("dif_made", st)
            h_turned = sem("h_turned", st)
            hT_ready = sem("hT_ready", st)
            row_asked = sem("row_asked", st)
            row_turned = sem("row_turned", st)
            produced = sem("produced", st)
            mid = sem("mid", st)
            spread_out = sem("spread_out", st)
            exped = sem("exped", st)
            summed = sem("summed", st)
            dst_ready = sem("dst_ready", st)
            old_landed = [sem(f"old_landed{k}", st) for k in range(2)]
            fold = sem("fold", st)
            faded = sem("faded", st)
            stored = sem("stored", st)
            block = st.enter_context(nc.Block())
            FRONT, MID, FOLD = 4, 14, 14

            DEPTH = 3

            @block.gpsimd
            def _(pool):
                def step(at):
                    a, m, b, c = at(0), at(1), at(2), at(3)
                    if c.live:
                        k = c.slot(2)
                        pool.wait_ge(mid, MID * (c.n + 1)) if False else None
                        if c.after(2):
                            pool.wait_ge(old_landed[k], 8 * (c.n - k))
                        pool.tensor_copy(gd[:, k], d_index[:, bass.ds(c.n, 1)]).then_inc(dst_ready, 1)
                        if c.after(1):
                            pool.wait_ge(stored, 16 * c.n)
                        pool.wait_ge(dst_ready, c.n + 1)
                        if c.after(2):
                            pool.wait_ge(fold, FOLD * (c.n - 1))
                        own_wait(pool)
                        pool.indirect_dma_start(old[:, k], None, table, bass.IndirectOffsetOnAxis(gd[:, k], 0)).then_inc(old_landed[k], 16)
                    if a.live:
                        k = a.slot(2)
                        if a.after(2):
                            pool.wait_ge(x_landed[k], 16 * (a.n - k))
                            pool.wait_ge(h_made, 2 * (a.n - 1))
                        pool.tensor_copy(gi[:, k], x_index[:, bass.ds(a.n, 1)].rearrange("p a b -> p (a b)")).then_inc(idx_ready, 1)
                        pool.wait_ge(idx_ready, a.n + 1)
                        own_wait(pool)
                        for j in range(2):
                            pool.indirect_dma_start(xg[:, k, j], None, x, bass.IndirectOffsetOnAxis(gi[:, k, j:j + 1], 0)).then_inc(x_landed[k], 16)
                    if m.live:
                        k = m.slot(2)
                        pool.wait_ge(front, FRONT * m.n + 2)
                        own_wait(pool)
                        pool.tensor_scalar(ve[:, k], mv[:, k, :, 1], EPS, None, ALU.add).then_inc(rooted, 1)
                        pool.wait_ge(rooted, 2 * m.n + 1)
                        pool.tensor_tensor(rstd[:, k], ve[:, k], half[:, 0:2], ALU.pow).then_inc(rooted, 1)
                        pool.wait_ge(h_made, 2 * (m.n + 1))
                        if m.after(2):
                            pool.wait_ge(h_turned, m.n - 1)
                        pool.tensor_tensor(hdif[:, k], hg[:, k, 0], hg[:, k, 1], ALU.subtract).then_inc(dif_made, 1)
                    if c.live:
                        k = c.slot(2)
                        pool.wait_ge(fold, FOLD * (c.n + 1))
                        own_wait(pool)
                        pool.indirect_dma_start(table, bass.IndirectOffsetOnAxis(si[:, k], 0), new[:, k], None).then_inc(stored, 16)
                pipeline(pool, step, C, DEPTH, 2)
                pool.wait_ge(stored, 16 * C)

            @block.scalar
            def _(act):
                def step(at):
                    m, b, c = at(1), at(2), at(3)
                    if b.live:
                        k = b.slot(2)
                        act.wait_ge(h_turned, b.n + 1)
                        if b.after(2):
                            act.wait_ge(produced, b.n - 1)
                        nc.scalar.activation(hT[:, k], pT[:], ACT.Copy).then_inc(hT_ready, 1)
                    if m.live:
                        k = m.slot(2)
                        act.wait_ge(front, FRONT * m.n + 4)
                        act.wait_ge(rooted, 2 * (m.n + 1))
                        if m.after(2):
                            act.wait_ge(dif_made, m.n - 1)
                            act.wait_ge(h_turned, m.n - 1)
                        for j in range(2):
                            nc.scalar.activation(hg[:, k, j], xg[:, k, j], ACT.Relu, bias=nmr[:, k, j:j + 1],
                                                 scale=rstd[:, k, j:j + 1]).then_inc(h_made, 1)
                    if b.live:
                        k = b.slot(2)
                        act.wait_ge(mid, MID * b.n + 12)
                        if b.after(1):
                            act.wait_ge(mid, MID * b.n)
                        if b.after(2):
                            act.wait_ge(summed, b.n - 1)
                        nc.scalar.activation(weighed[:, k, D:DH], shifted[:], ACT.Exp).then_inc(exped, 1)
                    if c.live:
                        act.wait_ge(fold, FOLD * c.n + 6)
                        nc.scalar.activation(fade[:], pair[:], ACT.Exp).then_inc(faded, 1)
                pipeline(act, step, C, DEPTH, 2)

            @block.tensor
            def _(pe):
                def step(at):
                    b = at(2)
                    if not b.live:
                        return
                    k = b.slot(2)
                    pe.wait_ge(dif_made, b.n + 1)
                    if b.after(1):
                        pe.wait_ge(hT_ready, b.n)
                    for j, h in enumerate((hdif[:, k], hg[:, k, 1])):
                        for c in range(KC):
                            ins = nc.tensor.transpose(pT[:, 2 * j + c], h[:, c * P:(c + 1) * P], ident[:])
                    ins.then_inc(h_turned, 1)
                    pe.wait_ge(row_asked, b.n + 1)
                    if b.after(1):
                        pe.wait_ge(mid, MID * b.n)
                    nc.tensor.transpose(pR[:, 0:P], dv[:, k, 0:1].broadcast_to([P, P]), ident[:]).then_inc(row_turned, 1)
                    pe.wait_ge(hT_ready, b.n + 1)
                    nc.tensor.matmul(pD[:, 0:DH], ones_row[:], bias_row[:], start=True, stop=False)
                    for c in range(KC):
                        nc.tensor.matmul(pD[:, 0:DH], hT[:, k, c], wd[:, c], start=False, stop=(c == KC - 1))
                    for c in range(KC):
                        ins = nc.tensor.matmul(pS[:, 0:H], hT[:, k, KC + c], wa[:, c], start=(c == 0), stop=(c == KC - 1))
                    ins.then_inc(produced, 1)
                    pe.wait_ge(mid, MID * b.n + 7)
                    for h in range(H):
                        ins = nc.tensor.transpose(pG[:, h], raw[:, 0, h:h + 1].broadcast_to([P, P]), ident[:])
                    ins.then_inc(spread_out, 1)
                    pe.wait_ge(mid, MID * (b.n + 1))
                    pe.wait_ge(exped, b.n + 1)
                    if b.after(2):
                        pe.wait_ge(fold, FOLD * (b.n - 1))
                    nc.tensor.matmul(pV[k][:, 0:DH], same[:, k], weighed[:, k], start=True, stop=True).then_inc(summed, 1)
                pipeline(pe, step, C, DEPTH, 2)

            @block.vector
            def _(dve):
                def step(at):
                    m, b, c = at(1), at(2), at(3)
                    if m.live:
                        k = m.slot(2)
                        dve.wait_ge(x_landed[k], 16 * (m.n - k) + 32)
                        if m.after(2):
                            dve.wait_ge(rooted, 2 * (m.n - 1))
                        for j in range(2):
                            ins = nc.vector.bn_stats(stats[:, k, j], xg[:, k, j])
                        ins.then_inc(front, 1)
                        dve.wait_ge(front, FRONT * m.n + 1)
                        own_wait(dve)
                        for j in range(2):
                            ins = nc.vector.bn_aggr(mv[:, k, j], stats[:, k, j])
                        ins.then_inc(front, 1)
                    if b.live:
                        k = b.slot(2)
                        M0 = MID * b.n
                        if b.after(2):
                            dve.wait_ge(summed, b.n - 1)
                        nc.vector.tensor_copy(dv[:, k], d_value[:, bass.ds(b.n, 1)].rearrange("p a b -> p (a b)")).then_inc(row_asked, 1)
                        dve.wait_ge(row_asked, b.n + 1)
                        dve.wait_ge(row_turned, b.n + 1)
                        nc.vector.tensor_scalar(same[:, k], pR[:, 0:P], dv[:, k, 0:1], None, ALU.is_equal).then_inc(mid, 1)
                        dve.wait_ge(mid, M0 + 1)
                        nc.vector.tensor_scalar(apart[:], same[:, k], 1.0, FAR, ALU.subtract, ALU.mult).then_inc(mid, 1)
                        nc.vector.tensor_tensor(lower[:], same[:, k], below[:], ALU.mult).then_inc(mid, 1)
                        dve.wait_ge(mid, M0 + 3)
                        nc.vector.tensor_reduce(dups[:], lower[:], AX_X, ALU.max).then_inc(mid, 1)
                        dve.wait_ge(mid, M0 + 4)
                        nc.vector.tensor_scalar(spare_if[:], dups[:], dv[:, k, 1:2], dv[:, k, 0:1], ALU.mult, ALU.add).then_inc(mid, 1)
                        dve.wait_ge(mid, M0 + 5)
                        if b.after(2):
                            dve.wait_ge(stored, 16 * (b.n - 1))
                        nc.vector.tensor_copy(si[:, k], spare_if[:]).then_inc(mid, 1)
                        dve.wait_ge(produced, b.n + 1)
                        nc.vector.tensor_copy(s_own[:, 0], pS[:, 0:H])
                        nc.vector.memset(raw[:, 1], 0.0)
                        nc.vector.tensor_copy(raw[:, 0], pD[:, D:DH]).then_inc(mid, 1)
                    if m.live:
                        k = m.slot(2)
                        dve.wait_ge(rooted, 2 * (m.n + 1))
                        if m.after(2):
                            dve.wait_ge(h_made, 2 * (m.n - 1))
                        nc.vector.scalar_tensor_tensor(nmr[:, k], mv[:, k, :, 0], -1.0, rstd[:, k], ALU.mult, ALU.mult).then_inc(front, 2)
                    if b.live:
                        k = b.slot(2)
                        dve.wait_ge(spread_out, b.n + 1)
                        nc.vector.tensor_tensor(spread[:], pG[:], apart[:].rearrange("p (a n) -> p a n", a=1).broadcast_to([P, H, P]), ALU.add).then_inc(mid, 1)
                        dve.wait_ge(mid, M0 + 8)
                        nc.vector.tensor_reduce(raw[:, 2], spread[:], AX_X, ALU.max).then_inc(mid, 1)
                        dve.wait_ge(mid, M0 + 9)
                        nc.vector.tensor_tensor(rawsum[:], raw[:], s_own[:].broadcast_to([P, 3, H]), ALU.add).then_inc(mid, 1)
                        dve.wait_ge(mid, M0 + 10)
                        nc.vector.scalar_tensor_tensor(score[:, k], rawsum[:], SLOPE, rawsum[:], ALU.mult, ALU.max).then_inc(mid, 1)
                        dve.wait_ge(mid, M0 + 11)
                        nc.vector.tensor_tensor(shifted[:], score[:, k, 0], score[:, k, 2], ALU.subtract).then_inc(mid, 1)
                        dve.wait_ge(exped, b.n + 1)
                        nc.vector.tensor_tensor(weighed[:, k, 0:D].rearrange("p (h d) -> p h d", h=H),
                                                pD[:, 0:D].rearrange("p (h d) -> p h d", h=H),
                                                weighed[:, k, D:DH].rearrange("p (h d) -> p h d", d=1).broadcast_to([P, H, HD]),
                                                ALU.mult).then_inc(mid, 2)
                    if c.live:
                        k = c.slot(2)
                        F0 = FOLD * c.n
                        lo, hi = old[:, k, D:DH], old[:, k, DH:NR]
                        dve.wait_ge(old_landed[k], 8 * (c.n - k) + 16)
                        if c.after(2):
                            dve.wait_ge(stored, 16 * (c.n - 1))
                        nc.vector.scalar_tensor_tensor(mine[:], hi, 0.0, score[:, k, 1], ALU.is_equal, ALU.mult).then_inc(fold, 1)
                        nc.vector.scalar_tensor_tensor(lold[:], hi, 0.0, hi, ALU.is_equal, ALU.add).then_inc(fold, 1)
                        dve.wait_ge(fold, F0 + 1)
                        nc.vector.tensor_tensor(pair[:, 0], mine[:], lo, ALU.add).then_inc(fold, 1)
                        dve.wait_ge(fold, F0 + 3)
                        nc.vector.tensor_tensor(new[:, k, D:DH], pair[:, 0], score[:, k, 2], ALU.max).then_inc(fold, 1)
                        dve.wait_ge(fold, F0 + 4)
                        nc.vector.tensor_tensor(pair[:, 0], pair[:, 0], new[:, k, D:DH], ALU.subtract).then_inc(fold, 1)
                        nc.vector.tensor_tensor(pair[:, 1], score[:, k, 2], new[:, k, D:DH], ALU.subtract).then_inc(fold, 1)
                        dve.wait_ge(faded, c.n + 1)
                        dve.wait_ge(summed, c.n + 1)
                        nc.vector.tensor_tensor(part[:, 0], lold[:], fade[:, 0], ALU.mult)
                        nc.vector.tensor_tensor(part[:, 1], pV[k][:, D:DH], fade[:, 1], ALU.mult).then_inc(fold, 1)
                        dve.wait_ge(fold, F0 + 7)
                        nc.vector.tensor_tensor(new[:, k, DH:NR], part[:, 0], part[:, 1], ALU.add).then_inc(fold, 1)
                        dve.wait_ge(fold, F0 + 8)
                        nc.vector.tensor_scalar(recip[:], new[:, k, DH:NR], 1e-16, None, ALU.add).then_inc(fold, 1)
                        dve.wait_ge(fold, F0 + 9)
                        nc.vector.reciprocal(recip[:], recip[:]).then_inc(fold, 1)
                        dve.wait_ge(fold, F0 + 10)
                        nc.vector.tensor_tensor(scale[:, 0], part[:, 0], recip[:], ALU.mult)
                        nc.vector.tensor_tensor(scale[:, 1], fade[:, 1], recip[:], ALU.mult).then_inc(fold, 1)
                        dve.wait_ge(fold, F0 + 11)
                        def per_head(ap):
                            return ap.rearrange("p (h d) -> p h d", h=H)

                        def widened(j):
                            return scale[:, j].rearrange("p (h d) -> p h d", d=1).broadcast_to([P, H, HD])
                        nc.vector.tensor_tensor(per_head(kept[:]), per_head(old[:, k, 0:D]), widened(0), ALU.mult)
                        nc.vector.tensor_tensor(per_head(added[:]), per_head(pV[k][:, 0:D]), widened(1), ALU.mult).then_inc(fold, 1)
                        dve.wait_ge(fold, F0 + 12)
                        nc.vector.tensor_tensor(new[:, k, 0:D], kept[:], added[:], ALU.add).then_inc(fold, 2)
                pipeline(dve, step, C, DEPTH, 2)

        with ExitStack() as st:
            xs = sb("xs", [P, 4, Q, D], F32, st)
            xb = sb("xb", [P, 4, Q, D], F32, st)
            msg = sb("msg", [P, 2, Q, D], F32, st)
            cen = sb("cen", [P, 2, Q, D], F32, st)
            cT = [sb(f"cT{k}", [P, 2, KC, CH], F32R, st) for k in range(2)]
            r = sb("r", [P, 2, Q, D], F32, st)
            rn = sb("rn", [P, 2, Q, D], F32, st)
            nT = [sb(f"nT{k}", [P, 2, KC, CH], F32R, st) for k in range(2)]
            up = sb("up", [P, 2, KC, CH], F32, st)
            uT = [sb(f"uT{k}", [P, 2, KC, CH], F32R, st) for k in range(2)]
            y = sb("y", [P, 2, Q, D], F32, st)
            sta = sb("sta", [P, 2, 2, Q, 6], F32, st)
            mvn = sb("mvn", [P, 2, 2, Q, 2], F32, st)
            ven = sb("ven", [P, 2, 2, Q], F32, st)
            rsn = sb("rsn", [P, 2, 2, Q], F32, st)
            nmn = sb("nmn", [P, 2, Q], F32, st)
            nm1 = sb("nm1", [P, 2, Q], F32, st)

            pt = ps("pt", [P, 2, 512], st)
            p1 = ps("p1", [P, 2, 512], st)
            p2 = ps("p2", [P, 2, 512], st)
            p3 = ps("p3", [P, 2, 512], st)

            xs_in = [sem(f"xs_in{k}", st) for k in range(4)]
            msg_in = [sem(f"msg_in{k}", st) for k in range(2)]
            y_out = [sem(f"y_out{k}", st) for k in range(2)]
            norm1 = sem("norm1", st)
            root1 = sem("root1", st)
            less1 = sem("less1", st)
            centred = sem("centred", st)
            xb_made = sem("xb_made", st)
            c_turned = sem("c_turned", st)
            cT_high = sem("cT_high", st)
            cT_low = sem("cT_low", st)
            times_w = sem("times_w", st)
            r_made = sem("r_made", st)
            norm2 = sem("norm2", st)
            root2 = sem("root2", st)
            shift2 = sem("shift2", st)
            rn_made = sem("rn_made", st)
            n_turned = sem("n_turned", st)
            nT_high = sem("nT_high", st)
            nT_low = sem("nT_low", st)
            times_w1 = sem("times_w1", st)
            up_made = sem("up_made", st)
            uT_high = sem("uT_high", st)
            uT_low = sem("uT_low", st)
            times_w2 = sem("times_w2", st)
            y_made = sem("y_made", st)
            block = st.enter_context(nc.Block())

            NORM1, ROOT, NORM2 = 2, 2, 2
            DEPTH = 4
            LEAD = 3

            def rows(of, at, cols):
                if at.looped:
                    first = at.n * CH
                else:
                    first = min(at.n * CH, N - CH)
                return of[bass.ds(first, CH), 0:cols].rearrange("(p q) n -> p q n", q=Q)

            @block.sync
            def _(sp):
                def step(at):
                    a, o = at(0), at(DEPTH + LEAD)
                    if a.live:
                        k = a.slot(4)
                        if a.after(4):
                            sp.wait_ge(xb_made, a.n - 3)
                            sp.wait_ge(centred, a.n - 3)
                        sp.dma_start(xs[:, k], rows(x, a, D)).then_inc(xs_in[k], 16)
                    g = at(1)
                    if g.live:
                        j = g.slot(2)
                        if g.after(2):
                            sp.wait_ge(r_made, Q * (g.n - 1))
                        sp.dma_start(msg[:, j], rows(table, g, D)).then_inc(msg_in[j], 16)
                    if o.live:
                        j = o.slot(2)
                        sp.wait_ge(y_made, 2 * (o.n + 1))
                        if not o.looped and o.n == NC - 1:
                            sp.wait_ge(y_out[1 - j], 16 * ((o.n - 1) // 2 + 1))
                        sp.dma_start(rows(out, o, D), y[:, j]).then_inc(y_out[j], 16)
                pipeline(sp, step, NC, DEPTH + LEAD, 4)
                for j in range(2):
                    sp.wait_ge(y_out[j], 16 * (NC // 2))

            @block.vector
            def _(dve):
                def step(at):
                    f, a, b, o = at(0), at(1), at(3), at(5)
                    if f.live:
                        k, j = f.slot(4), f.slot(2)
                        dve.wait_ge(xs_in[k], 4 * (f.n - k) + 16)
                        if f.after(2):
                            dve.wait_ge(root1, ROOT * (f.n - 1))
                            dve.wait_ge(centred, f.n - 1)
                        for q in range(Q):
                            ins = nc.vector.bn_stats(sta[:, j, 0, q], xs[:, k, q])
                        ins.then_inc(norm1, 1)
                        dve.wait_ge(norm1, NORM1 * f.n + 1)
                        own_wait(dve)
                        for q in range(Q):
                            ins = nc.vector.bn_aggr(mvn[:, j, 0, q], sta[:, j, 0, q])
                        ins.then_inc(norm1, 1)
                    if a.live:
                        j = a.slot(2)
                        for c in range(KC):
                            dve.wait_ge(cT_high, 2 * a.n + c + 1)
                            if a.after(2) and c == 0:
                                dve.wait_ge(times_w, 2 * (a.n - 1))
                            nc.vector.tensor_tensor(cT[1][:, j, c], pt[:, c], cT[0][:, j, c].bitcast(F32), ALU.subtract).then_inc(cT_low, 1)
                    if o.live:
                        j, k = o.slot(2), o.slot(4)
                        dve.wait_ge(xb_made, o.n + 1)
                        if o.after(2):
                            dve.wait_ge(y_out[j], 8 * (o.n - j))
                        for c in range(2):
                            dve.wait_ge(times_w2, 2 * o.n + c + 1)
                            nc.vector.tensor_tensor(y[:, j, 2 * c:2 * c + 2], p3[:, c].rearrange("p (q n) -> p q n", q=2),
                                                    xb[:, k, 2 * c:2 * c + 2], ALU.add).then_inc(y_made, 1)
                    if b.live:
                        j = b.slot(2)
                        for c in range(KC):
                            dve.wait_ge(nT_high, 2 * b.n + c + 1)
                            if b.after(2) and c == 0:
                                dve.wait_ge(times_w1, 2 * (b.n - 1))
                            nc.vector.tensor_tensor(nT[1][:, j, c], pt[:, c], nT[0][:, j, c].bitcast(F32), ALU.subtract).then_inc(nT_low, 1)
                    if a.live:
                        j = a.slot(2)
                        dve.wait_ge(msg_in[j], 8 * (a.n - j) + 16)
                        if a.after(2):
                            dve.wait_ge(rn_made, a.n - 1)
                        for q in range(Q):
                            if q % 2 == 0:
                                dve.wait_ge(times_w, 2 * a.n + q // 2 + 1)
                            nc.vector.scalar_tensor_tensor(r[:, j, q], p1[:, q // 2, (q % 2) * D:(q % 2 + 1) * D],
                                                           rsn[:, j, 0, q:q + 1], msg[:, j, q], ALU.mult, ALU.add).then_inc(r_made, 1)
                        for q in range(Q):
                            dve.wait_ge(r_made, Q * a.n + q + 1)
                            ins = nc.vector.bn_stats(sta[:, j, 1, q], r[:, j, q])
                        ins.then_inc(norm2, 1)
                        dve.wait_ge(norm2, NORM2 * a.n + 1)
                        if a.after(2):
                            dve.wait_ge(root2, ROOT * (a.n - 1))
                        own_wait(dve)
                        for q in range(Q):
                            ins = nc.vector.bn_aggr(mvn[:, j, 1, q], sta[:, j, 1, q])
                        ins.then_inc(norm2, 1)
                pipeline(dve, step, NC, DEPTH + 1, 4)

            @block.gpsimd
            def _(pool):
                def step(at):
                    f, a, b, g, u = at(0), at(1), at(2), at(2), at(4)
                    if f.live:
                        k, j = f.slot(4), f.slot(2)
                        pool.wait_ge(norm1, NORM1 * (f.n + 1))
                        if f.after(2):
                            pool.wait_ge(r_made, Q * (f.n - 1))
                        own_wait(pool)
                        pool.tensor_scalar(ven[:, j, 0], mvn[:, j, 0, :, 1], EPS, None, ALU.add).then_inc(root1, 1)
                        pool.wait_ge(root1, ROOT * f.n + 1)
                        pool.tensor_tensor(rsn[:, j, 0], ven[:, j, 0], half[:, 0:Q], ALU.pow).then_inc(root1, 1)
                        if f.after(2):
                            pool.wait_ge(centred, f.n - 1)
                        own_wait(pool)
                        pool.tensor_scalar(nm1[:, j], mvn[:, j, 0, :, 0], -1.0, None, ALU.mult).then_inc(less1, 1)
                    if u.live:
                        j = u.slot(2)
                        for c in range(KC):
                            pool.wait_ge(uT_high, 2 * u.n + c + 1)
                            if u.after(2) and c == 0:
                                pool.wait_ge(times_w2, 2 * (u.n - 1))
                            pool.tensor_tensor(uT[1][:, j, c], up[:, j, c], uT[0][:, j, c].bitcast(F32), ALU.subtract).then_inc(uT_low, 1)
                    if g.live:
                        j = g.slot(2)
                        pool.wait_ge(norm2, NORM2 * (g.n + 1))
                        if g.after(2):
                            pool.wait_ge(rn_made, g.n - 1)
                        own_wait(pool)
                        pool.tensor_scalar(ven[:, j, 1], mvn[:, j, 1, :, 1], EPS, None, ALU.add).then_inc(root2, 1)
                        pool.wait_ge(root2, ROOT * g.n + 1)
                        pool.tensor_tensor(rsn[:, j, 1], ven[:, j, 1], half[:, 0:Q], ALU.pow).then_inc(root2, 1)
                        pool.wait_ge(root2, ROOT * g.n + 2)
                        pool.tensor_tensor(nmn[:, j], mvn[:, j, 1, :, 0], rsn[:, j, 1], ALU.mult).then_inc(shift2, 1)
                        pool.wait_ge(shift2, 2 * g.n + 1)
                        own_wait(pool)
                        pool.tensor_scalar(nmn[:, j], nmn[:, j], -1.0, None, ALU.mult).then_inc(shift2, 1)
                    if a.live:
                        k = a.slot(4)
                        if a.after(4):
                            pool.wait_ge(y_made, 2 * (a.n - 3))
                        pool.tensor_tensor(xb[:, k], xs[:, k], b2b[:].rearrange("p (a n) -> p a n", a=1).broadcast_to([P, Q, D]), ALU.add).then_inc(xb_made, 1)
                pipeline(pool, step, NC, DEPTH + 1, 4)

            @block.scalar
            def _(act):
                def step(at):
                    f, a, g, b = at(0), at(1), at(2), at(3)
                    if f.live:
                        k, j = f.slot(4), f.slot(2)
                        act.wait_ge(less1, f.n + 1)
                        if f.after(2):
                            act.wait_ge(c_turned, 2 * (f.n - 1))
                        for q in range(Q):
                            ins = nc.scalar.activation(cen[:, j, q], xs[:, k, q], ACT.Relu, bias=nm1[:, j, q:q + 1])
                        ins.then_inc(centred, 1)
                    if a.live:
                        j = a.slot(2)
                        for c in range(KC):
                            act.wait_ge(c_turned, 2 * a.n + c + 1)
                            if a.after(2) and c == 0:
                                act.wait_ge(times_w, 2 * (a.n - 1))
                                act.wait_ge(cT_low, 2 * (a.n - 1))
                            nc.scalar.activation(cT[0][:, j, c], pt[:, c], ACT.Copy).then_inc(cT_high, 1)
                    if b.live:
                        j = b.slot(2)
                        for c in range(KC):
                            act.wait_ge(n_turned, 2 * b.n + c + 1)
                            if b.after(2) and c == 0:
                                act.wait_ge(times_w1, 2 * (b.n - 1))
                                act.wait_ge(nT_low, 2 * (b.n - 1))
                            nc.scalar.activation(nT[0][:, j, c], pt[:, c], ACT.Copy).then_inc(nT_high, 1)
                    if g.live:
                        j = g.slot(2)
                        act.wait_ge(shift2, 2 * (g.n + 1))
                        if g.after(2):
                            act.wait_ge(n_turned, 2 * (g.n - 1))
                        for q in range(Q):
                            ins = nc.scalar.activation(rn[:, j, q], r[:, j, q], ACT.Identity, bias=nmn[:, j, q:q + 1], scale=rsn[:, j, 1, q:q + 1])
                        ins.then_inc(rn_made, 1)
                    if b.live:
                        j = b.slot(2)
                        if b.after(2):
                            act.wait_ge(uT_low, 2 * (b.n - 1))
                            act.wait_ge(times_w2, 2 * (b.n - 1))
                        for c in range(KC):
                            act.wait_ge(times_w1, 2 * b.n + c + 1)
                            nc.scalar.activation(up[:, j, c], p2[:, c], ACT.Relu, bias=b1e[:, c:c + 1]).then_inc(up_made, 1)
                        for c in range(KC):
                            act.wait_ge(up_made, 2 * b.n + c + 1)
                            nc.scalar.activation(uT[0][:, j, c], up[:, j, c], ACT.Copy).then_inc(uT_high, 1)
                pipeline(act, step, NC, DEPTH + 1, 4)

            @block.tensor
            def _(pe):
                THREE = ((0, 0), (1, 0), (0, 1))

                def step(at):
                    a, b, o = at(1), at(3), at(5)
                    if a.live:
                        j = a.slot(2)
                        pe.wait_ge(centred, a.n + 1)
                        if a.after(3):
                            pe.wait_ge(nT_low, 2 * (a.n - 2))
                        elif a.after(1):
                            pe.wait_ge(cT_low, 2 * a.n)
                        for c in range(KC):
                            for q in range(Q):
                                ins = nc.tensor.transpose(pt[:, c, q * P:(q + 1) * P], cen[:, j, q, c * P:(c + 1) * P], ident[:])
                            ins.then_inc(c_turned, 1)
                    if o.live:
                        j = o.slot(2)
                        pe.wait_ge(uT_low, 2 * (o.n + 1))
                        if o.after(1):
                            pe.wait_ge(y_made, 2 * o.n)
                        for q in range(Q):
                            for n, (d, e) in enumerate(THREE):
                                for c in range(KC):
                                    ins = nc.tensor.matmul(p3[:, q // 2, (q % 2) * D:(q % 2 + 1) * D], uT[d][:, j, c, q * P:(q + 1) * P],
                                                           w2p[e][:, c], start=(n == 0 and c == 0), stop=(n == 2 and c == KC - 1))
                            if q % 2:
                                ins.then_inc(times_w2, 1)
                    if b.live:
                        j = b.slot(2)
                        pe.wait_ge(rn_made, b.n + 1)
                        pe.wait_ge(cT_low, 2 * (b.n + 3) if b.looped else 2 * min(b.n + 3, NC))
                        for c in range(KC):
                            for q in range(Q):
                                ins = nc.tensor.transpose(pt[:, c, q * P:(q + 1) * P], rn[:, j, q, c * P:(c + 1) * P], ident[:])
                            ins.then_inc(n_turned, 1)
                    if a.live:
                        j = a.slot(2)
                        pe.wait_ge(cT_low, 2 * (a.n + 1))
                        if a.after(1):
                            pe.wait_ge(r_made, Q * a.n)
                        for q in range(Q):
                            for n, (d, e) in enumerate(THREE):
                                for c in range(KC):
                                    ins = nc.tensor.matmul(p1[:, q // 2, (q % 2) * D:(q % 2 + 1) * D], cT[d][:, j, c, q * P:(q + 1) * P],
                                                           wi[e][:, c], start=(n == 0 and c == 0), stop=(n == 2 and c == KC - 1))
                            if q % 2:
                                ins.then_inc(times_w, 1)
                    if b.live:
                        j = b.slot(2)
                        pe.wait_ge(nT_low, 2 * (b.n + 1))
                        if b.after(1):
                            pe.wait_ge(up_made, 2 * b.n)
                        for o_ in range(KC):
                            for n, (d, e) in enumerate(THREE):
                                for c in range(KC):
                                    ins = nc.tensor.matmul(p2[:, o_], w1p[e][:, c, o_ * P:(o_ + 1) * P], nT[d][:, j, c],
                                                           start=(n == 0 and c == 0), stop=(n == 2 and c == KC - 1))
                            ins.then_inc(times_w1, 1)
                pipeline(pe, step, NC, DEPTH + 1, 4)


_INS = ["x", "src", "dst", "L0_gnn_W", "L0_gnn_att_src", "L0_gnn_att_dst", "L0_gnn_bias", "L0_gnn_ln_g",
        "L0_gnn_ln_b", "L0_gnn_W1", "L0_gnn_b1", "L0_gnn_W2", "L0_gnn_b2"]


def build_program(nc, arrays):
    args = [nc.dram_tensor(f"in_{name}", arrays[f"in_{name}"].shape, mybir.dt.from_np(arrays[f"in_{name}"].dtype),
                           kind="ExternalInput").ap() for name in _INS]
    out = nc.dram_tensor("out_0", arrays["in_x"].shape, F32, kind="ExternalOutput").ap()
    gat_kernel(nc, *args, out)


def kernel(**inputs):
    import numpy as _np
    import concourse.bacc as _bacc
    from concourse.bass_utils import run_bass_kernel_spmd as _run

    nc = _bacc.Bacc("TRN2", target_bir_lowering=False, num_devices=1)
    arrays = {f"in_{name}": _np.ascontiguousarray(inputs[name]) for name in _INS}
    build_program(nc, arrays)
    r = _run(nc, [arrays], core_ids=[0])
    return r.results[0]["out_0"]
```

```python
from contextlib import ExitStack

import concourse.bass as bass
from concourse import mybir

P = 128
F32 = mybir.dt.float32
F32R = mybir.dt.float32r
BF16 = mybir.dt.bfloat16
I32 = mybir.dt.int32
ALU = mybir.AluOpType
ACT = mybir.ActivationFunctionType
AX_X = mybir.AxisListType.X
EPS = 1e-5
SLOPE = 0.2
FAR = 1e30


class Place:

    def __init__(self, number, slot_of, live, looped):
        self.n = number
        self.slot_of = slot_of
        self.live = live
        self.looped = looped

    def slot(self, slots):
        return self.slot_of % slots

    def after(self, k):
        return self.looped or self.n >= k


def pipeline(eng, step, tiles, depth, unroll):
    first = -(-(depth + unroll) // unroll) * unroll
    last = (tiles - 1) // unroll * unroll

    def fixed(s):
        step(lambda lag: Place(s - lag, s - lag + 16 * unroll, 0 <= s - lag < tiles, False))

    for s in range(first):
        fixed(s)
    with eng.Fori(0, (last - first) // unroll) as turn:
        i = turn * unroll + first
        for u in range(unroll):
            step(lambda lag, u=u: Place(i + (u - lag), u - lag + 16 * unroll, True, True))
    for s in range(last, tiles + depth):
        fixed(s)


def gat_kernel(nc, x, src, dst, w, att_src, att_dst, bias, ln_g, ln_b, w1, b1, w2, b2, out):
    N, D = x.shape
    (E,) = src.shape
    H, HD = att_src.shape
    KC = D // P
    C = -(-E // P)
    FULL = E // C
    REST = E - FULL * C
    NR = D + 2 * H
    DH = D + H
    TR = 16
    NB = -(-(N + 2 * P) // (P * TR))
    NT = NB * P * TR
    NONE = N + P
    EARLY = min(8, NB - 1)
    Q = 4
    CH = P * Q
    NC = -(-N // CH)
    READS = 5
    UNUSED = NONE + 1
    assert KC == 2 and FULL == P - 1 and C % 4 == 0 and NC % 4 == 0 and NT > UNUSED

    table = nc.dram_tensor("table", [NT, NR], F32, kind="Internal").ap()

    with ExitStack() as whole:
        def sem(name, stack=whole):
            return stack.enter_context(nc.semaphore(name))

        def sb(name, shape, dt=F32, stack=whole):
            return stack.enter_context(nc.sbuf_tensor(name, shape, dt))

        def ps(name, shape, stack):
            return stack.enter_context(nc.psum_tensor(name, shape, F32))

        passed = {nc.vector: sem("passed_vector"), nc.gpsimd: sem("passed_gpsimd"), nc.scalar: sem("passed_scalar")}

        def own_wait(eng):
            eng.sem_inc(passed[eng])

        ident = sb("ident", [P, P])
        below = sb("below", [P, P])
        half = sb("half", [P, 8])
        wd = sb("wd", [P, KC, DH])
        wa = sb("wa", [P, KC, H])
        bias_row = [sb(f"bias_row{k}", [1, DH], F32R) for k in range(2)]
        ones_row = sb("ones_row", [1, P], F32R)
        ones = sb("ones", [P, P])
        identb = sb("identb", [P, P], BF16)
        wi = [sb(f"wi{k}", [P, KC, D], F32R) for k in range(2)]
        w1p = [sb(f"w1p{k}", [P, KC, D], F32R) for k in range(2)]
        w2p = [sb(f"w2p{k}", [P, KC, D], F32R) for k in range(2)]
        b1e = sb("b1e", [P, KC])
        b2b = sb("b2b", [P, D])
        index = sb("index", [P, C + READS, 4], I32)
        x_index, rows_index = index[:, 0:C, 0:2], index[:, READS:, 2:4]
        d_value = sb("d_value", [P, C, 3])
        fill = sb("fill", [P, TR, NR])
        spare = sb("spare", [P, 1])
        filled = sem("filled")

        def fill_table(sp, first, end):
            rows = table.rearrange("(b p r) n -> b p (r n)", p=P, r=TR)
            with sp.Fori(first, end) as b:
                sp.dma_start(rows[bass.ds(b, 1)].rearrange("a p n -> (a p) n"), fill[:].rearrange("p r n -> p (r n)")).then_inc(filled, 16)

        with ExitStack() as st:
            wf = sb("wf", [P, KC, D], F32, st)
            w1f = sb("w1f", [P, KC, D], F32, st)
            w2f = sb("w2f", [P, KC, D], F32, st)
            wplus = sb("wplus", [P, KC, D], F32, st)
            w1g = sb("w1g", [P, KC, D], F32, st)
            prod = sb("prod", [P, KC, 2, D], F32, st)
            att = sb("att", [P, 2, D], F32, st)
            wad = sb("wad", [P, KC, 2, H], F32, st)
            gcol = sb("gcol", [P, KC], F32, st)
            lbcol = sb("lbcol", [P, KC], F32, st)
            b1col = sb("b1col", [P, KC], F32, st)
            biasb = sb("biasb", [P, D], F32, st)
            bias_f = sb("bias_f", [1, DH], F32, st)
            ones_f = sb("ones_f", [1, P], F32, st)
            s_in = sb("s_in", [P, C], I32, st)
            d_index = sb("d_index", [P, C], I32, st)
            sparei = sb("sparei", [P, 1], I32, st)
            pb = ps("pb", [P, KC, 512], st)
            padded = sem("padded", st)
            loaded = sem("loaded", st)
            indexed = sem("indexed", st)
            made = sem("made", st)
            folded = sem("folded", st)
            split = sem("split", st)
            turned0 = sem("turned0", st)
            fill_ready = sem("fill_ready", st)
            block = st.enter_context(nc.Block())

            @block.sync
            def _(sp):
                by_row = "(c p) n -> p c n"
                sp.dma_start(biasb[:], bias.rearrange("(a n) -> a n", a=1).broadcast_to([P, D])).then_inc(loaded, 16)
                sp.dma_start(wf[:], w.rearrange(by_row, p=P)).then_inc(loaded, 16)
                sp.dma_start(w1f[:], w1.rearrange(by_row, p=P)).then_inc(loaded, 16)
                sp.dma_start(w2f[:], w2.rearrange(by_row, p=P)).then_inc(loaded, 16)
                for k, a in enumerate((att_src, att_dst)):
                    sp.dma_start(att[:, k], a.rearrange("(a h) d -> a (h d)", a=1).broadcast_to([P, D])).then_inc(loaded, 16)
                sp.dma_start(b2b[:], b2.rearrange("(a n) -> a n", a=1).broadcast_to([P, D])).then_inc(loaded, 16)
                for col, v in ((gcol, ln_g), (lbcol, ln_b), (b1col, b1)):
                    for c in range(KC):
                        sp.dma_start(col[:, c:c + 1], v[c * P:(c + 1) * P].rearrange("(p a) -> p a", a=1)).then_inc(loaded, 16)
                sp.wait_ge(padded, 2)
                for tile, v in ((s_in, src), (d_index, dst)):
                    sp.dma_start(tile[0:FULL, :], v[0:FULL * C].rearrange("(p t) -> p t", t=C)).then_inc(indexed, 16)
                    sp.dma_start(tile[FULL:P, 0:REST], v[FULL * C:E].rearrange("(p t) -> p t", p=1)).then_inc(indexed, 16)
                sp.wait_ge(fill_ready, 1)
                fill_table(sp, 0, EARLY)

            @block.gpsimd
            def _(pool):
                pool.memset(s_in[:], 0).then_inc(padded, 1)
                pool.memset(d_index[:], NONE).then_inc(padded, 1)
                pool.memset(index[:, C:, 0:2], 0)
                pool.memset(index[:, 0:READS, 2:4], 0)
                pool.memset(ident[:], 0.0)
                pool.memset(below[:], 1.0)
                pool.memset(half[:], -0.5)
                pool.memset(ones_f[:], 1.0)
                pool.memset(ones[:], 1.0)
                pool.iota(sparei[:], pattern=[[0, 1]], base=N, channel_multiplier=1).then_inc(made, 1)
                pool.wait_ge(made, 1)
                pool.affine_select(out=ident[:], in_=ident[:], compare_op=ALU.not_equal, fill=1.0, base=0,
                                   pattern=[[-1, P]], channel_multiplier=1)
                pool.affine_select(out=below[:], in_=below[:], compare_op=ALU.is_gt, fill=0.0, base=0,
                                   pattern=[[-1, P]], channel_multiplier=1).then_inc(made, 1)

            @block.vector
            def _(dve):
                dve.wait_ge(loaded, 16 * 13)
                nc.vector.tensor_copy(fill[:, :, 0:D], biasb[:].rearrange("p (a n) -> p a n", a=1).broadcast_to([P, TR, D]))
                nc.vector.memset(fill[:, :, D:NR], 0.0).then_inc(fill_ready, 1)
                nc.vector.tensor_copy(bias_f[:, 0:D], biasb[0:1, :])
                nc.vector.memset(bias_f[:, D:DH], 0.0)
                for c in range(KC):
                    nc.vector.tensor_scalar(w1g[:, c], w1f[:, c], gcol[:, c:c + 1], None, ALU.mult)
                nc.vector.tensor_copy(wd[:, :, 0:D], wf[:])
                for c in range(KC):
                    for k in range(2):
                        ins = nc.vector.tensor_tensor(prod[:, c, k], wf[:, c], att[:, k], ALU.mult)
                ins.then_inc(folded, 1)
                dve.wait_ge(folded, 1)
                nc.vector.tensor_reduce(wad[:], prod[:].rearrange("p c k (h d) -> p c k h d", h=H), AX_X, ALU.add).then_inc(folded, 1)
                dve.wait_ge(made, 2)
                nc.vector.tensor_copy(wplus[:], wf[:])
                nc.vector.tensor_copy(identb[:], ident[:])
                nc.vector.tensor_copy(ones_row[:], ones_f[:])
                nc.vector.tensor_copy(bias_row[0][:], bias_f[:])
                nc.vector.tensor_copy(spare[:], sparei[:]).then_inc(folded, 1)
                dve.wait_ge(folded, 3)
                nc.vector.tensor_copy(wd[:, :, D:DH], wad[:, :, 0])
                nc.vector.tensor_tensor(wa[:], wad[:, :, 0], wad[:, :, 1], ALU.add)
                for c in range(KC):
                    diagonal = wplus[:, c, c * P:(c + 1) * P]
                    ins = nc.vector.tensor_tensor(diagonal, diagonal, ident[:], ALU.add)
                ins.then_inc(folded, 1)
                dve.wait_ge(indexed, 64)
                nc.vector.tensor_copy(x_index[:, :, 0], s_in[:])
                nc.vector.tensor_scalar(x_index[:, :, 1], d_index[:], float(N - 1), None, ALU.min)
                nc.vector.tensor_copy(d_value[:, :, 0], d_index[:]).then_inc(folded, 1)
                nc.vector.tensor_tensor(bias_row[1][:], bias_f[:], bias_row[0][:].bitcast(F32), ALU.subtract)
                dve.wait_ge(split, 3)
                for parts, whole_w in ((wi, wplus), (w1p, w1g), (w2p, w2f)):
                    nc.vector.tensor_tensor(parts[1][:], whole_w[:], parts[0][:].bitcast(F32), ALU.subtract)
                dve.wait_ge(turned0, 1)
                nc.vector.tensor_tensor(b1e[:], pb[:, :, 0], b1col[:], ALU.add).then_inc(folded, 1)

            @block.scalar
            def _(act):
                act.wait_ge(folded, 4)
                for parts, whole_w in ((wi, wplus), (w1p, w1g), (w2p, w2f)):
                    nc.scalar.activation(parts[0][:], whole_w[:], ACT.Copy).then_inc(split, 1)

            @block.tensor
            def _(pe):
                pe.wait_ge(loaded, 16 * 13)
                for o in range(KC):
                    for c in range(KC):
                        ins = nc.tensor.matmul(pb[:, o, 0:1], w1f[:, c, o * P:(o + 1) * P], lbcol[:, c:c + 1],
                                               start=(c == 0), stop=(c == KC - 1))
                ins.then_inc(turned0, 1)

        both = whole.enter_context(ExitStack())
        shared = sb("shared", [P, C, P], BF16, both)

        with ExitStack() as st:
            dcol = sb("dcol", [P, 4, 1], F32, st)
            hit = sb("hit", [P, 2, P], F32, st)
            dups = sb("dups", [P, C], F32, st)
            again = sb("again", [P, C], F32, st)
            moved = sb("moved", [P, 2, C], F32, st)
            pR4 = ps("pR4", [P, 4, 512], st)
            col_ready = sem("col_ready", st)
            col_turned = sem("col_turned", st)
            compared = sem("compared", st)
            bulk = sem("bulk", st)
            block = st.enter_context(nc.Block())

            @block.sync
            def _(sp):
                fill_table(sp, EARLY, NB)

            @block.tensor
            def _(pe):
                def step(at):
                    t = at(0)
                    if t.live:
                        k = t.slot(4)
                        pe.wait_ge(col_ready, t.n + 1)
                        if t.after(4):
                            pe.wait_ge(compared, 2 * (t.n - 2))
                        nc.tensor.transpose(pR4[:, k, 0:P], dcol[:, k].broadcast_to([P, P]), ident[:]).then_inc(col_turned, 1)
                pipeline(pe, step, C, 0, 4)

            @block.vector
            def _(dve):
                nc.vector.memset(again[:, 0:1], 0.0)

                def step(at):
                    t, b = at(0), at(2)
                    if t.live:
                        k = t.slot(4)
                        if t.after(4):
                            dve.wait_ge(col_turned, t.n - 3)
                            dve.wait_ge(compared, 2 * (t.n - 3))
                        nc.vector.tensor_copy(dcol[:, k], d_value[:, bass.ds(t.n, 1), 0]).then_inc(col_ready, 1)
                    if b.live:
                        k, l = b.slot(4), b.slot_of + 3
                        dve.wait_ge(col_turned, b.n + 1)
                        if b.after(1):
                            dve.wait_ge(compared, 2 * b.n)
                            nc.vector.scalar_tensor_tensor(hit[:, 1], pR4[:, l % 4, 0:P], dcol[:, k, 0:1], ones[:], ALU.is_equal, ALU.mult,
                                                           accum_out=again[:, bass.ds(b.n, 1)]).then_inc(compared, 1)
                        else:
                            nc.vector.memset(hit[:, 1], 0.0).then_inc(compared, 1)
                        nc.vector.tensor_scalar(shared[:, bass.ds(b.n, 1)].rearrange("p a n -> p (a n)"), pR4[:, k, 0:P], dcol[:, k, 0:1], None,
                                                ALU.is_equal)
                        nc.vector.scalar_tensor_tensor(hit[:, 0], pR4[:, k, 0:P], dcol[:, k, 0:1], below[:], ALU.is_equal, ALU.mult,
                                                       accum_out=dups[:, bass.ds(b.n, 1)]).then_inc(compared, 1)
                pipeline(dve, step, C, 2, 4)
                dve.wait_ge(compared, 2 * C)
                d = d_value[:, :, 0]
                nc.vector.tensor_scalar(dups[:], dups[:], 1.0, None, ALU.min)
                nc.vector.tensor_scalar(again[:], again[:], 1.0, None, ALU.min)
                nc.vector.tensor_scalar(moved[:, 0], d, -1.0, spare[:, 0:1], ALU.mult, ALU.add)
                nc.vector.tensor_scalar(moved[:, 1], d, -1.0, float(UNUSED), ALU.mult, ALU.add).then_inc(bulk, 1)
                dve.wait_ge(bulk, 1)
                nc.vector.tensor_tensor(moved[:, 0], moved[:, 0], dups[:], ALU.mult)
                nc.vector.tensor_tensor(moved[:, 1], moved[:, 1], again[:], ALU.mult).then_inc(bulk, 1)
                dve.wait_ge(bulk, 2)
                nc.vector.tensor_tensor(rows_index[:, :, 1], moved[:, 0], d, ALU.add)
                nc.vector.tensor_tensor(rows_index[:, :, 0], moved[:, 1], d, ALU.add)
                nc.vector.tensor_scalar(d_value[:, :, 1], dups[:], -1.0, 1.0, ALU.mult, ALU.add)
                nc.vector.tensor_scalar(d_value[:, :, 2], again[:], -1.0, 1.0, ALU.mult, ALU.add)

        with ExitStack() as st:
            taken = sb("taken", [P, 4, 4], I32, st)
            xg = sb("xg", [P, 4, 2, D], F32, st)
            stats = sb("stats", [P, 2, 2, 6], F32, st)
            mv = sb("mv", [P, 2, 2, 2], F32, st)
            ve = sb("ve", [P, 2, 2], F32, st)
            rstd = sb("rstd", [P, 2, 2], F32, st)
            nmr = sb("nmr", [P, 2, 2], F32, st)
            hg = sb("hg", [P, 2, 2, D], F32, st)
            hdif = sb("hdif", [P, 2, D], F32, st)
            hT = sb("hT", [P, 2, 4, P], F32, st)
            dv = sb("dv", [P, 4, 3], F32, st)
            same = sb("same", [P, 4, P], F32, st)
            link = sb("link", [P, 4, P], F32, st)
            apart = sb("apart", [P, 2, P], BF16, st)
            raw = sb("raw", [P, 2, 3, H], F32, st)
            s_own = sb("s_own", [P, 2, 1, H], F32, st)
            rawsum = sb("rawsum", [P, 3, H], F32, st)
            top = sb("top", [P, 2, H], F32, st)
            shifted = sb("shifted", [P, H], F32, st)
            weighed = sb("weighed", [P, 2, DH], F32, st)
            old = sb("old", [P, 2, NR], F32, st)
            cur = sb("cur", [P, 2, NR + 3 * H], F32, st)
            new = sb("new", [P, 2, NR], F32, st)
            pair = sb("pair", [P, 3, H], F32, st)
            fade = sb("fade", [P, 3, H], F32, st)
            part = sb("part", [P, 3, H], F32, st)
            before = sb("before", [P, H], F32, st)
            recip = sb("recip", [P, H], F32, st)
            scale = sb("scale", [P, 2, H], F32, st)
            kept = sb("kept", [P, D], F32, st)
            added = sb("added", [P, D], F32, st)

            pT = ps("pT", [P, 4, P], st)
            pR = ps("pR", [P, 512], st)
            pD = [ps(f"pD{k}", [P, 512], st) for k in range(2)]
            pG = ps("pG", [P, H, P], st)
            pV = ps("pV", [P, 512], st)
            pF = ps("pF", [P, 512], st)

            idx_ready = sem("idx_ready", st)
            x_landed = [sem(f"x_landed{k}", st) for k in range(4)]
            stats_taken = sem("stats_taken", st)
            normed = sem("normed", st)
            eps_added = sem("eps_added", st)
            rooted = sem("rooted", st)
            shift_ready = sem("shift_ready", st)
            h_made = sem("h_made", st)
            dif_made = sem("dif_made", st)
            dv_ready = sem("dv_ready", st)
            row_turned = sem("row_turned", st)
            same_ready = sem("same_ready", st)
            linked = sem("linked", st)
            apart_ready = sem("apart_ready", st)
            h_turned = sem("h_turned", st)
            hT_ready = sem("hT_ready", st)
            produced = sem("produced", st)
            raw_ready = sem("raw_ready", st)
            spread_out = sem("spread_out", st)
            largest = sem("largest", st)
            scored = sem("scored", st)
            exped = sem("exped", st)
            weighed_ready = sem("weighed_ready", st)
            summed = sem("summed", st)
            old_landed = [sem(f"old_landed{k}", st) for k in range(2)]
            handed_on = sem("handed_on", st)
            merge = sem("merge", st)
            faded = sem("faded", st)
            stored = sem("stored", st)
            zeroed = sem("zeroed", st)
            block = st.enter_context(nc.Block())
            MERGE, SCORE = 10, 3

            DEPTH = 7

            def per_head(ap):
                return ap.rearrange("p (h d) -> p h d", h=H)

            def widened(ap):
                return ap.rearrange("p (h d) -> p h d", d=1).broadcast_to([P, H, HD])

            @block.gpsimd
            def _(pool):
                def take(s):
                    pool.tensor_copy(taken[:, s.slot(4)], index[:, bass.ds(s.n, 1)].rearrange("p a b -> p (a b)")).then_inc(idx_ready, 1)

                take(Place(0, 0, True, False))

                def step(at):
                    ahead, g, m, h, r, e = at(-1), at(0), at(1), at(2), at(READS), at(7)
                    if e.live:
                        k = e.slot(2)
                        pool.wait_ge(merge, MERGE * (e.n + 1))
                        if e.after(1):
                            pool.wait_ge(stored, 16 * e.n)
                        own_wait(pool)
                        pool.indirect_dma_start(table, bass.IndirectOffsetOnAxis(taken[:, (e.slot_of + READS) % 4, 3:4], 0), new[:, k], None).then_inc(stored, 16)
                    if g.live:
                        k = g.slot(4)
                        pool.wait_ge(idx_ready, g.n + 1)
                        own_wait(pool)
                        for j in range(2):
                            pool.indirect_dma_start(xg[:, k, j], None, x, bass.IndirectOffsetOnAxis(taken[:, k, j:j + 1], 0)).then_inc(x_landed[k], 16)
                    if r.live:
                        k = r.slot(2)
                        if r.after(2):
                            pool.wait_ge(stored, 16 * (r.n - 1))
                            pool.wait_ge(merge, MERGE * (r.n - 2) + 1)
                        else:
                            pool.wait_ge(filled, 16 * NB)
                        pool.wait_ge(idx_ready, r.n + READS + 1)
                        own_wait(pool)
                        pool.indirect_dma_start(old[:, k], None, table, bass.IndirectOffsetOnAxis(taken[:, (r.slot_of + READS) % 4, 2:3], 0)).then_inc(old_landed[k], 16)
                    if ahead.looped or ahead.n < C + READS:
                        if ahead.after(4):
                            pool.wait_ge(h_made, 2 * (ahead.n - 3 if ahead.looped else min(ahead.n - 3, C)))
                            own_wait(pool)
                        take(ahead)
                    if h.live:
                        k = h.slot(2)
                        pool.wait_ge(h_made, 2 * (h.n + 1))
                        if h.after(2):
                            pool.wait_ge(h_turned, h.n - 1)
                        pool.tensor_tensor(hdif[:, k], hg[:, k, 0], hg[:, k, 1], ALU.subtract).then_inc(dif_made, 1)
                    if m.live:
                        k = m.slot(2)
                        pool.wait_ge(eps_added, m.n + 1)
                        if m.after(2):
                            pool.wait_ge(h_made, 2 * (m.n - 1))
                        pool.tensor_tensor(rstd[:, k], ve[:, k], half[:, 0:2], ALU.pow).then_inc(rooted, 1)
                pipeline(pool, step, C, DEPTH, 4)
                pool.wait_ge(stored, 16 * C)

            @block.scalar
            def _(act):
                def step(at):
                    h, a, w, c = at(2), at(3), at(5), at(6)
                    if h.live:
                        k = h.slot(2)
                        act.wait_ge(shift_ready, h.n + 1)
                        if h.after(2):
                            act.wait_ge(dif_made, h.n - 1)
                            act.wait_ge(h_turned, h.n - 1)
                        for j in range(2):
                            nc.scalar.activation(hg[:, k, j], xg[:, h.slot(4), j], ACT.Relu, bias=nmr[:, k, j:j + 1],
                                                 scale=rstd[:, k, j:j + 1]).then_inc(h_made, 1)
                    if w.live:
                        k = w.slot(2)
                        act.wait_ge(scored, SCORE * (w.n + 1))
                        if w.after(2):
                            act.wait_ge(summed, w.n - 1)
                        nc.scalar.activation(weighed[:, k, D:DH], shifted[:], ACT.Exp).then_inc(exped, 1)
                    if c.live:
                        act.wait_ge(merge, MERGE * c.n + 3)
                        nc.scalar.activation(fade[:], pair[:], ACT.Exp).then_inc(faded, 1)
                    if a.live:
                        k = a.slot(2)
                        act.wait_ge(h_turned, a.n + 1)
                        if a.after(2):
                            act.wait_ge(produced, a.n - 1)
                        nc.scalar.activation(hT[:, k], pT[:], ACT.Copy).then_inc(hT_ready, 1)
                        if a.after(2):
                            act.wait_ge(spread_out, a.n - 1)
                        if a.after(4):
                            act.wait_ge(summed, a.n - 3)
                            own_wait(act)
                        in_tile = shared[:, bass.ds(a.n, 1)].rearrange("p a n -> p (a n)")
                        nc.scalar.activation(same[:, a.slot(4)], in_tile, ACT.Copy).then_inc(same_ready, 1)
                        nc.scalar.activation(apart[:, k], in_tile, ACT.Copy, bias=-FAR, scale=FAR).then_inc(apart_ready, 1)
                        act.wait_ge(produced, a.n + 1)
                        if a.after(2):
                            act.wait_ge(scored, SCORE * (a.n - 1))
                        nc.scalar.activation(raw[:, k, 2], pD[k][:, D:DH], ACT.Copy).then_inc(raw_ready, 1)
                        nc.scalar.activation(s_own[:, k, 0], pD[k][:, DH:DH + H], ACT.Copy).then_inc(raw_ready, 1)
                pipeline(act, step, C, DEPTH, 4)

            @block.tensor
            def _(pe):
                def step(at):
                    a, b, w, c = at(3), at(4), at(5), at(6)
                    if c.live and c.after(1):
                        k = c.slot(2)
                        pe.wait_ge(merge, MERGE * c.n)
                        pe.wait_ge(linked, c.n)
                        nc.tensor.matmul(pF[:, 0:NR], link[:, c.slot(4)], new[:, 1 - k], start=True, stop=True).then_inc(handed_on, 1)
                    if a.live:
                        k = a.slot(2)
                        pe.wait_ge(dv_ready, a.n + 1)
                        if a.after(2):
                            pe.wait_ge(linked, a.n - 1)
                        nc.tensor.transpose(pR[:, 0:P], dv[:, a.slot(4), 0:1].broadcast_to([P, P]), ident[:]).then_inc(row_turned, 1)
                        pe.wait_ge(dif_made, a.n + 1)
                        if a.after(1):
                            pe.wait_ge(hT_ready, a.n)
                        for j, h in enumerate((hdif[:, k], hg[:, k, 1])):
                            for c_ in range(KC):
                                ins = nc.tensor.transpose(pT[:, 2 * j + c_], h[:, c_ * P:(c_ + 1) * P], ident[:])
                        ins.then_inc(h_turned, 1)
                    if b.live:
                        k = b.slot(2)
                        pe.wait_ge(apart_ready, b.n + 1)
                        pe.wait_ge(raw_ready, 2 * (b.n + 1))
                        if b.after(1):
                            pe.wait_ge(largest, b.n)
                        for h in range(H):
                            nc.tensor.matmul(pG[:, h], identb[:], apart[:, k], start=True, stop=False)
                            ins = nc.tensor.matmul(pG[:, h], raw[:, k, 2, h:h + 1].broadcast_to([P, P]), ident[:], start=False, stop=True)
                        ins.then_inc(spread_out, 1)
                    if a.live:
                        k = a.slot(2)
                        if a.after(2):
                            pe.wait_ge(weighed_ready, a.n - 1)
                            pe.wait_ge(raw_ready, 2 * (a.n - 1))
                        for n in range(2):
                            nc.tensor.matmul(pD[k][:, 0:DH], ones_row[:], bias_row[n][:], start=(n == 0), stop=False)
                        pe.wait_ge(hT_ready, a.n + 1)
                        for c_ in range(KC):
                            nc.tensor.matmul(pD[k][:, 0:DH], hT[:, k, c_], wd[:, c_], start=False, stop=(c_ == KC - 1))
                        for c_ in range(KC):
                            ins = nc.tensor.matmul(pD[k][:, DH:DH + H], hT[:, k, KC + c_], wa[:, c_], start=(c_ == 0), stop=(c_ == KC - 1))
                        ins.then_inc(produced, 1)
                    if w.live:
                        k = w.slot(2)
                        pe.wait_ge(weighed_ready, w.n + 1)
                        pe.wait_ge(same_ready, w.n + 1)
                        if w.after(1):
                            pe.wait_ge(merge, MERGE * (w.n - 1) + 9)
                        nc.tensor.matmul(pV[:, 0:DH], same[:, w.slot(4)], weighed[:, k], start=True, stop=True).then_inc(summed, 1)
                pipeline(pe, step, C, DEPTH, 4)

            @block.vector
            def _(dve):
                nc.vector.memset(raw[:, :, 0], 0.0).then_inc(zeroed, 1)
                dve.wait_ge(zeroed, 1)

                def step(at):
                    m, h, a, b, w, c = at(1), at(2), at(3), at(4), at(5), at(6)
                    kw, kc = w.slot(2), c.slot(2)
                    M0, S0 = MERGE * c.n, SCORE * w.n
                    row = cur[:, kc]
                    if h.live:
                        k = h.slot(2)
                        dve.wait_ge(rooted, h.n + 1)
                        if h.after(2):
                            dve.wait_ge(h_made, 2 * (h.n - 1))
                        nc.vector.scalar_tensor_tensor(nmr[:, k], mv[:, k, :, 0], -1.0, rstd[:, k], ALU.mult, ALU.mult).then_inc(shift_ready, 1)
                    if w.live:
                        dve.wait_ge(largest, w.n + 1)
                        dve.wait_ge(raw_ready, 2 * (w.n + 1))
                        nc.vector.tensor_tensor(rawsum[:], raw[:, kw], s_own[:, kw].broadcast_to([P, 3, H]), ALU.add).then_inc(scored, 1)
                    if m.live:
                        k = m.slot(2)
                        dve.wait_ge(x_landed[m.slot(4)], 8 * (m.n - m.slot(4)) + 32)
                        nc.vector.bn_stats(stats[:, k, 0], xg[:, m.slot(4), 0])
                    if w.live:
                        dve.wait_ge(scored, S0 + 1)
                        nc.vector.scalar_tensor_tensor(cur[:, kw, NR:].rearrange("p (a h) -> p a h", h=H), rawsum[:], SLOPE, rawsum[:],
                                                       ALU.mult, ALU.max).then_inc(scored, 1)
                    if c.live:
                        dve.wait_ge(old_landed[kc], 8 * (c.n - kc) + 16)
                        if c.after(1):
                            dve.wait_ge(handed_on, c.n)
                            nc.vector.scalar_tensor_tensor(row[:, 0:NR], old[:, kc], dv[:, c.slot(4), 2:3], pF[:, 0:NR], ALU.mult, ALU.add).then_inc(merge, 1)
                        else:
                            nc.vector.tensor_copy(row[:, 0:NR], old[:, kc]).then_inc(merge, 1)
                    if w.live:
                        dve.wait_ge(scored, S0 + 2)
                        nc.vector.tensor_tensor(shifted[:], cur[:, kw, NR + 2 * H:], cur[:, kw, NR + H:NR + 2 * H], ALU.subtract)
                        nc.vector.tensor_tensor(top[:, kw], cur[:, kw, NR:NR + H], cur[:, kw, NR + H:NR + 2 * H], ALU.max).then_inc(scored, 1)
                    if c.live:
                        dve.wait_ge(merge, M0 + 1)
                        dve.wait_ge(scored, SCORE * (c.n + 1))
                        if c.after(2):
                            dve.wait_ge(stored, 16 * (c.n - 1))
                        nc.vector.tensor_tensor(new[:, kc, DH:NR], row[:, DH:NR], top[:, kc], ALU.max).then_inc(merge, 1)
                    if c.live:
                        dve.wait_ge(merge, M0 + 2)
                        nc.vector.tensor_tensor(pair[:], row[:, DH:NR + 2 * H].rearrange("p (a h) -> p a h", h=H),
                                                new[:, kc, DH:NR].rearrange("p (a h) -> p a h", a=1).broadcast_to([P, 3, H]),
                                                ALU.subtract).then_inc(merge, 1)
                    if w.live:
                        dve.wait_ge(exped, w.n + 1)
                        nc.vector.tensor_tensor(per_head(weighed[:, kw, 0:D]), per_head(pD[kw][:, 0:D]), widened(weighed[:, kw, D:DH]),
                                                ALU.mult).then_inc(weighed_ready, 1)
                    if c.live:
                        dve.wait_ge(faded, c.n + 1)
                        nc.vector.tensor_tensor(part[:, 0], row[:, D:DH], fade[:, 0], ALU.mult)
                        nc.vector.scalar_tensor_tensor(part[:, 1], row[:, D:DH], 0.0, fade[:, 1], ALU.is_equal, ALU.mult)
                        dve.wait_ge(summed, c.n + 1)
                        nc.vector.tensor_tensor(part[:, 2], pV[:, D:DH], fade[:, 2], ALU.mult).then_inc(merge, 1)
                    if a.live and a.after(1):
                        dve.wait_ge(row_turned, a.n + 1)
                        if a.after(5):
                            dve.wait_ge(handed_on, a.n - 4)
                        p = dv[:, (a.slot_of + 3) % 4]
                        nc.vector.tensor_scalar(link[:, a.slot(4)], pR[:, 0:P], p[:, 0:1], p[:, 1:2], ALU.is_equal, ALU.mult).then_inc(linked, 1)
                    if c.live:
                        dve.wait_ge(merge, M0 + 4)
                        nc.vector.tensor_tensor(before[:], part[:, 0], part[:, 1], ALU.add).then_inc(merge, 1)
                    if h.live:
                        if h.after(4):
                            dve.wait_ge(row_turned, h.n - 3)
                        nc.vector.tensor_copy(dv[:, h.slot(4)], d_value[:, bass.ds(h.n, 1)].rearrange("p a b -> p (a b)")).then_inc(dv_ready, 1)
                    if c.live:
                        dve.wait_ge(merge, M0 + 5)
                        nc.vector.scalar_tensor_tensor(new[:, kc, D:DH], before[:], 1e-16, part[:, 2], ALU.add, ALU.add).then_inc(merge, 1)
                        dve.wait_ge(merge, M0 + 6)
                        nc.vector.reciprocal(recip[:], new[:, kc, D:DH]).then_inc(merge, 1)
                        dve.wait_ge(merge, M0 + 7)
                        nc.vector.tensor_tensor(scale[:, 0], before[:], recip[:], ALU.mult)
                        nc.vector.tensor_tensor(scale[:, 1], fade[:, 2], recip[:], ALU.mult).then_inc(merge, 1)
                    if m.live:
                        k = m.slot(2)
                        nc.vector.bn_stats(stats[:, k, 1], xg[:, m.slot(4), 1]).then_inc(stats_taken, 1)
                    if c.live:
                        dve.wait_ge(merge, M0 + 8)
                        nc.vector.tensor_tensor(per_head(kept[:]), per_head(row[:, 0:D]), widened(scale[:, 0]), ALU.mult)
                        nc.vector.tensor_tensor(per_head(added[:]), per_head(pV[:, 0:D]), widened(scale[:, 1]), ALU.mult).then_inc(merge, 1)
                    if m.live:
                        k = m.slot(2)
                        dve.wait_ge(stats_taken, m.n + 1)
                        own_wait(dve)
                        for j in range(2):
                            ins = nc.vector.bn_aggr(mv[:, k, j], stats[:, k, j])
                        ins.then_inc(normed, 1)
                    if c.live:
                        dve.wait_ge(merge, M0 + 9)
                        nc.vector.tensor_tensor(new[:, kc, 0:D], kept[:], added[:], ALU.add).then_inc(merge, 1)
                    if m.live:
                        k = m.slot(2)
                        dve.wait_ge(normed, m.n + 1)
                        if m.after(2):
                            dve.wait_ge(rooted, m.n - 1)
                        nc.vector.tensor_scalar(ve[:, k], mv[:, k, :, 1], EPS, None, ALU.add).then_inc(eps_added, 1)
                    if b.live:
                        dve.wait_ge(spread_out, b.n + 1)
                        nc.vector.tensor_reduce(raw[:, b.slot(2), 1], pG[:], AX_X, ALU.max).then_inc(largest, 1)
                pipeline(dve, step, C, DEPTH, 4)

        both.close()

        with ExitStack() as st:
            xs = sb("xs", [P, 4, Q, D], F32, st)
            xb = sb("xb", [P, 4, Q, D], F32, st)
            msg = sb("msg", [P, 2, Q, D], F32, st)
            cen = sb("cen", [P, 2, Q, D], F32, st)
            cT = [sb(f"cT{k}", [P, 2, KC, CH], F32R, st) for k in range(2)]
            r = sb("r", [P, 2, Q, D], F32, st)
            rn = sb("rn", [P, 2, Q, D], F32, st)
            nT = [sb(f"nT{k}", [P, 2, KC, CH], F32R, st) for k in range(2)]
            up = sb("up", [P, 2, KC, CH], F32, st)
            uT = [sb(f"uT{k}", [P, 2, KC, CH], F32R, st) for k in range(2)]
            y = sb("y", [P, 2, Q, D], F32, st)
            sta = sb("sta", [P, 2, 2, Q, 6], F32, st)
            mvn = sb("mvn", [P, 2, 2, Q, 2], F32, st)
            ven = sb("ven", [P, 2, 2, Q], F32, st)
            rsn = sb("rsn", [P, 2, 2, Q], F32, st)
            nmn = sb("nmn", [P, 2, Q], F32, st)
            nm1 = sb("nm1", [P, 2, Q], F32, st)

            pt = ps("pt", [P, 2, 512], st)
            p1 = ps("p1", [P, 2, 512], st)
            p2 = ps("p2", [P, 2, 512], st)
            p3 = ps("p3", [P, 2, 512], st)

            xs_in = [sem(f"xs_in{k}", st) for k in range(4)]
            msg_in = [sem(f"msg_in{k}", st) for k in range(2)]
            y_out = [sem(f"y_out{k}", st) for k in range(2)]
            norm1 = sem("norm1", st)
            root1 = sem("root1", st)
            less1 = sem("less1", st)
            centred = sem("centred", st)
            xb_made = sem("xb_made", st)
            c_turned = sem("c_turned", st)
            cT_high = sem("cT_high", st)
            cT_low = sem("cT_low", st)
            times_w = sem("times_w", st)
            r_made = sem("r_made", st)
            norm2 = sem("norm2", st)
            root2 = sem("root2", st)
            shift2 = sem("shift2", st)
            rn_made = sem("rn_made", st)
            n_turned = sem("n_turned", st)
            nT_high = sem("nT_high", st)
            nT_low = sem("nT_low", st)
            times_w1 = sem("times_w1", st)
            up_made = sem("up_made", st)
            uT_high = sem("uT_high", st)
            uT_low = sem("uT_low", st)
            times_w2 = sem("times_w2", st)
            y_made = sem("y_made", st)
            block = st.enter_context(nc.Block())

            NORM1, ROOT, NORM2 = 2, 2, 2
            DEPTH = 6
            LEAD = 2

            def rows(of, at, cols):
                if at.looped:
                    first = at.n * CH
                else:
                    first = min(at.n * CH, N - CH)
                return of[bass.ds(first, CH), 0:cols].rearrange("(p q) n -> p q n", q=Q)

            @block.sync
            def _(sp):
                def step(at):
                    a, o = at(0), at(DEPTH + LEAD)
                    if a.live:
                        k = a.slot(4)
                        if a.after(4):
                            sp.wait_ge(xb_made, a.n - 3)
                            sp.wait_ge(centred, a.n - 3)
                        sp.dma_start(xs[:, k], rows(x, a, D)).then_inc(xs_in[k], 16)
                    g = at(2)
                    if g.live:
                        j = g.slot(2)
                        if g.after(2):
                            sp.wait_ge(r_made, Q * (g.n - 1))
                        sp.dma_start(msg[:, j], rows(table, g, D)).then_inc(msg_in[j], 16)
                    if o.live:
                        j = o.slot(2)
                        sp.wait_ge(y_made, 2 * (o.n + 1))
                        if not o.looped and o.n == NC - 1:
                            sp.wait_ge(y_out[1 - j], 16 * ((o.n - 1) // 2 + 1))
                        sp.dma_start(rows(out, o, D), y[:, j]).then_inc(y_out[j], 16)
                pipeline(sp, step, NC, DEPTH + LEAD, 4)
                for j in range(2):
                    sp.wait_ge(y_out[j], 16 * (NC // 2))

            @block.vector
            def _(dve):
                def step(at):
                    f, a, b, o = at(0), at(2), at(4), at(6)
                    if a.live:
                        j = a.slot(2)
                        for c in range(KC):
                            dve.wait_ge(cT_high, 2 * a.n + c + 1)
                            if a.after(2) and c == 0:
                                dve.wait_ge(times_w, 2 * (a.n - 1))
                            nc.vector.tensor_tensor(cT[1][:, j, c], pt[:, c], cT[0][:, j, c].bitcast(F32), ALU.subtract).then_inc(cT_low, 1)
                    if f.live:
                        k, j = f.slot(4), f.slot(2)
                        dve.wait_ge(xs_in[k], 4 * (f.n - k) + 16)
                        if f.after(2):
                            dve.wait_ge(root1, ROOT * (f.n - 1))
                            dve.wait_ge(centred, f.n - 1)
                        for q in range(Q):
                            ins = nc.vector.bn_stats(sta[:, j, 0, q], xs[:, k, q])
                        ins.then_inc(norm1, 1)
                        dve.wait_ge(norm1, NORM1 * f.n + 1)
                        own_wait(dve)
                        for q in range(Q):
                            ins = nc.vector.bn_aggr(mvn[:, j, 0, q], sta[:, j, 0, q])
                        ins.then_inc(norm1, 1)
                    if b.live:
                        j = b.slot(2)
                        for c in range(KC):
                            dve.wait_ge(nT_high, 2 * b.n + c + 1)
                            if b.after(2) and c == 0:
                                dve.wait_ge(times_w1, 2 * (b.n - 1))
                            nc.vector.tensor_tensor(nT[1][:, j, c], pt[:, c], nT[0][:, j, c].bitcast(F32), ALU.subtract).then_inc(nT_low, 1)
                    if o.live:
                        j, k = o.slot(2), o.slot(4)
                        dve.wait_ge(xb_made, o.n + 1)
                        if o.after(2):
                            dve.wait_ge(y_out[j], 8 * (o.n - j))
                        for c in range(2):
                            dve.wait_ge(times_w2, 2 * o.n + c + 1)
                            nc.vector.tensor_tensor(y[:, j, 2 * c:2 * c + 2], p3[:, c].rearrange("p (q n) -> p q n", q=2),
                                                    xb[:, k, 2 * c:2 * c + 2], ALU.add).then_inc(y_made, 1)
                    if a.live:
                        j = a.slot(2)
                        dve.wait_ge(msg_in[j], 8 * (a.n - j) + 16)
                        if a.after(2):
                            dve.wait_ge(rn_made, a.n - 1)
                        for q in range(Q):
                            if q % 2 == 0:
                                dve.wait_ge(times_w, 2 * a.n + q // 2 + 1)
                            nc.vector.scalar_tensor_tensor(r[:, j, q], p1[:, q // 2, (q % 2) * D:(q % 2 + 1) * D],
                                                           rsn[:, j, 0, q:q + 1], msg[:, j, q], ALU.mult, ALU.add).then_inc(r_made, 1)
                        for q in range(Q):
                            dve.wait_ge(r_made, Q * a.n + q + 1)
                            ins = nc.vector.bn_stats(sta[:, j, 1, q], r[:, j, q])
                        ins.then_inc(norm2, 1)
                        dve.wait_ge(norm2, NORM2 * a.n + 1)
                        if a.after(2):
                            dve.wait_ge(shift2, 2 * (a.n - 1))
                        own_wait(dve)
                        for q in range(Q):
                            ins = nc.vector.bn_aggr(mvn[:, j, 1, q], sta[:, j, 1, q])
                        ins.then_inc(norm2, 1)
                pipeline(dve, step, NC, DEPTH, 4)

            @block.gpsimd
            def _(pool):
                def step(at):
                    f, a, g, u = at(1), at(2), at(3), at(5)
                    if f.live:
                        k, j = f.slot(4), f.slot(2)
                        pool.wait_ge(norm1, NORM1 * (f.n + 1))
                        if f.after(2):
                            pool.wait_ge(r_made, Q * (f.n - 1))
                        own_wait(pool)
                        pool.tensor_scalar(ven[:, j, 0], mvn[:, j, 0, :, 1], EPS, None, ALU.add).then_inc(root1, 1)
                        pool.wait_ge(root1, ROOT * f.n + 1)
                        pool.tensor_tensor(rsn[:, j, 0], ven[:, j, 0], half[:, 0:Q], ALU.pow).then_inc(root1, 1)
                        if f.after(2):
                            pool.wait_ge(centred, f.n - 1)
                        own_wait(pool)
                        pool.tensor_scalar(nm1[:, j], mvn[:, j, 0, :, 0], -1.0, None, ALU.mult).then_inc(less1, 1)
                    if g.live:
                        j = g.slot(2)
                        pool.wait_ge(norm2, NORM2 * (g.n + 1))
                        if g.after(2):
                            pool.wait_ge(rn_made, g.n - 1)
                        own_wait(pool)
                        pool.tensor_scalar(ven[:, j, 1], mvn[:, j, 1, :, 1], EPS, None, ALU.add).then_inc(root2, 1)
                        pool.wait_ge(root2, ROOT * g.n + 1)
                        pool.tensor_tensor(rsn[:, j, 1], ven[:, j, 1], half[:, 0:Q], ALU.pow).then_inc(root2, 1)
                        pool.wait_ge(root2, ROOT * g.n + 2)
                        pool.tensor_tensor(nmn[:, j], mvn[:, j, 1, :, 0], rsn[:, j, 1], ALU.mult).then_inc(shift2, 1)
                        pool.wait_ge(shift2, 2 * g.n + 1)
                        own_wait(pool)
                        pool.tensor_scalar(nmn[:, j], nmn[:, j], -1.0, None, ALU.mult).then_inc(shift2, 1)
                    if u.live:
                        j = u.slot(2)
                        for c in range(KC):
                            pool.wait_ge(uT_high, 2 * u.n + c + 1)
                            if u.after(2) and c == 0:
                                pool.wait_ge(times_w2, 2 * (u.n - 1))
                            pool.tensor_tensor(uT[1][:, j, c], up[:, j, c], uT[0][:, j, c].bitcast(F32), ALU.subtract).then_inc(uT_low, 1)
                    if a.live:
                        k = a.slot(4)
                        if a.after(4):
                            pool.wait_ge(y_made, 2 * (a.n - 3))
                        pool.tensor_tensor(xb[:, k], xs[:, k], b2b[:].rearrange("p (a n) -> p a n", a=1).broadcast_to([P, Q, D]), ALU.add).then_inc(xb_made, 1)
                pipeline(pool, step, NC, DEPTH, 4)

            @block.scalar
            def _(act):
                def step(at):
                    f, a, g, b, u = at(1), at(2), at(3), at(4), at(5)
                    if a.live:
                        j = a.slot(2)
                        for c in range(KC):
                            act.wait_ge(c_turned, 2 * a.n + c + 1)
                            if a.after(2) and c == 0:
                                act.wait_ge(times_w, 2 * (a.n - 1))
                                act.wait_ge(cT_low, 2 * (a.n - 1))
                            nc.scalar.activation(cT[0][:, j, c], pt[:, c], ACT.Copy).then_inc(cT_high, 1)
                    if u.live:
                        j = u.slot(2)
                        if u.after(2):
                            act.wait_ge(uT_low, 2 * (u.n - 1))
                            act.wait_ge(times_w2, 2 * (u.n - 1))
                        for c in range(KC):
                            act.wait_ge(times_w1, 2 * u.n + c + 1)
                            nc.scalar.activation(up[:, j, c], p2[:, c], ACT.Relu, bias=b1e[:, c:c + 1]).then_inc(up_made, 1)
                        for c in range(KC):
                            act.wait_ge(up_made, 2 * u.n + c + 1)
                            nc.scalar.activation(uT[0][:, j, c], up[:, j, c], ACT.Copy).then_inc(uT_high, 1)
                    if b.live:
                        j = b.slot(2)
                        for c in range(KC):
                            act.wait_ge(n_turned, 2 * b.n + c + 1)
                            if b.after(2) and c == 0:
                                act.wait_ge(times_w1, 2 * (b.n - 1))
                                act.wait_ge(nT_low, 2 * (b.n - 1))
                            nc.scalar.activation(nT[0][:, j, c], pt[:, c], ACT.Copy).then_inc(nT_high, 1)
                    if g.live:
                        j = g.slot(2)
                        act.wait_ge(shift2, 2 * (g.n + 1))
                        if g.after(2):
                            act.wait_ge(n_turned, 2 * (g.n - 1))
                        for q in range(Q):
                            ins = nc.scalar.activation(rn[:, j, q], r[:, j, q], ACT.Identity, bias=nmn[:, j, q:q + 1], scale=rsn[:, j, 1, q:q + 1])
                        ins.then_inc(rn_made, 1)
                    if f.live:
                        k, j = f.slot(4), f.slot(2)
                        act.wait_ge(less1, f.n + 1)
                        if f.after(2):
                            act.wait_ge(c_turned, 2 * (f.n - 1))
                        for q in range(Q):
                            ins = nc.scalar.activation(cen[:, j, q], xs[:, k, q], ACT.Relu, bias=nm1[:, j, q:q + 1])
                        ins.then_inc(centred, 1)
                pipeline(act, step, NC, DEPTH, 4)

            @block.tensor
            def _(pe):
                THREE = ((0, 0), (1, 0), (0, 1))

                def step(at):
                    a, b, o = at(2), at(4), at(6)
                    if a.live:
                        j = a.slot(2)
                        pe.wait_ge(centred, a.n + 1)
                        if a.after(3):
                            pe.wait_ge(nT_low, 2 * (a.n - 2))
                        elif a.after(1):
                            pe.wait_ge(cT_low, 2 * a.n)
                        for c in range(KC):
                            for q in range(Q):
                                ins = nc.tensor.transpose(pt[:, c, q * P:(q + 1) * P], cen[:, j, q, c * P:(c + 1) * P], ident[:])
                            ins.then_inc(c_turned, 1)
                    if o.live:
                        j = o.slot(2)
                        pe.wait_ge(uT_low, 2 * (o.n + 1))
                        if o.after(1):
                            pe.wait_ge(y_made, 2 * o.n)
                        for q in range(Q):
                            for n, (d, e) in enumerate(THREE):
                                for c in range(KC):
                                    ins = nc.tensor.matmul(p3[:, q // 2, (q % 2) * D:(q % 2 + 1) * D], uT[d][:, j, c, q * P:(q + 1) * P],
                                                           w2p[e][:, c], start=(n == 0 and c == 0), stop=(n == 2 and c == KC - 1))
                            if q % 2:
                                ins.then_inc(times_w2, 1)
                    if b.live:
                        j = b.slot(2)
                        pe.wait_ge(rn_made, b.n + 1)
                        pe.wait_ge(cT_low, 2 * (b.n + 3) if b.looped else 2 * min(b.n + 3, NC))
                        for c in range(KC):
                            for q in range(Q):
                                ins = nc.tensor.transpose(pt[:, c, q * P:(q + 1) * P], rn[:, j, q, c * P:(c + 1) * P], ident[:])
                            ins.then_inc(n_turned, 1)
                    if a.live:
                        j = a.slot(2)
                        pe.wait_ge(cT_low, 2 * (a.n + 1))
                        if a.after(1):
                            pe.wait_ge(r_made, Q * a.n)
                        for q in range(Q):
                            for n, (d, e) in enumerate(THREE):
                                for c in range(KC):
                                    ins = nc.tensor.matmul(p1[:, q // 2, (q % 2) * D:(q % 2 + 1) * D], cT[d][:, j, c, q * P:(q + 1) * P],
                                                           wi[e][:, c], start=(n == 0 and c == 0), stop=(n == 2 and c == KC - 1))
                            if q % 2:
                                ins.then_inc(times_w, 1)
                    if b.live:
                        j = b.slot(2)
                        pe.wait_ge(nT_low, 2 * (b.n + 1))
                        if b.after(1):
                            pe.wait_ge(up_made, 2 * b.n)
                        for o_ in range(KC):
                            for n, (d, e) in enumerate(THREE):
                                for c in range(KC):
                                    ins = nc.tensor.matmul(p2[:, o_], w1p[e][:, c, o_ * P:(o_ + 1) * P], nT[d][:, j, c],
                                                           start=(n == 0 and c == 0), stop=(n == 2 and c == KC - 1))
                            ins.then_inc(times_w1, 1)
                pipeline(pe, step, NC, DEPTH, 4)


_INS = ["x", "src", "dst", "L0_gnn_W", "L0_gnn_att_src", "L0_gnn_att_dst", "L0_gnn_bias", "L0_gnn_ln_g",
        "L0_gnn_ln_b", "L0_gnn_W1", "L0_gnn_b1", "L0_gnn_W2", "L0_gnn_b2"]


def build_program(nc, arrays):
    args = [nc.dram_tensor(f"in_{name}", arrays[f"in_{name}"].shape, mybir.dt.from_np(arrays[f"in_{name}"].dtype),
                           kind="ExternalInput").ap() for name in _INS]
    out = nc.dram_tensor("out_0", arrays["in_x"].shape, F32, kind="ExternalOutput").ap()
    gat_kernel(nc, *args, out)


def kernel(**inputs):
    import numpy as _np
    import concourse.bacc as _bacc
    from concourse.bass_utils import run_bass_kernel_spmd as _run

    nc = _bacc.Bacc("TRN2", target_bir_lowering=False, num_devices=1)
    arrays = {f"in_{name}": _np.ascontiguousarray(inputs[name]) for name in _INS}
    build_program(nc, arrays)
    r = _run(nc, [arrays], core_ids=[0])
    return r.results[0]["out_0"]
```
